# Optimizing a Trainium2 kernel written in Bass

```python
import numpy as np
import jax
import jax.numpy as jnp

def _softmax(x, axis=-1):
    return jax.nn.softmax(x, axis=axis)

def _gelu(x):
    return jax.nn.gelu(x, approximate=True)

def _silu(x):
    return jax.nn.silu(x)

def _sigmoid(x):
    return jax.nn.sigmoid(x)

def _layernorm(x, axis=-1, eps=1e-05):
    m = jnp.mean(x, axis=axis, keepdims=True)
    v = jnp.var(x, axis=axis, keepdims=True)
    return (x - m) / jnp.sqrt(v + eps)

def _scatter_add(tgt, idx, src, axis=0):
    return tgt.at[idx].add(src)

def _segment_sum(src, seg, n):
    return jax.ops.segment_sum(src, seg, n)
kernel_name = 'mk_cond_resid_d4_seqx_r8_33adcc'

def setup_inputs(seed: int=0):
    np.random.seed(seed)
    _w = jnp.asarray

    def _rec_inputs():
        import jax
        import jax.numpy as jnp
        _rk = jax.random.key(seed)
        x = -7.109e-05 + 0.9999 * jax.random.normal(jax.random.fold_in(_rk, 1), (64, 32, 512), jnp.float32)
        _lenS = 32 - jax.random.randint(jax.random.fold_in(_rk, 7), (64,), 0, max(1, 32 // 4) + 1, jnp.int32)
        _lenS2 = 32 - jax.random.randint(jax.random.fold_in(_rk, 8), (64,), 0, max(1, 32 // 4) + 1, jnp.int32)
        itok_B_0_15 = jax.random.randint(jax.random.fold_in(_rk, 11), (64,), 0, 16, jnp.int32)
        itok_B_6_15 = jax.random.randint(jax.random.fold_in(_rk, 12), (64,), 6, 16, jnp.int32)
        itok_Bx16_0_63 = jax.random.randint(jax.random.fold_in(_rk, 13), (64, 16), 0, 64, jnp.int32)
        itok_B_207_1644 = jax.random.randint(jax.random.fold_in(_rk, 14), (64,), 207, 1645, jnp.int32)
        return (x, itok_B_0_15, itok_B_6_15, itok_Bx16_0_63, itok_B_207_1644)
    x, itok_B_0_15, itok_B_6_15, itok_Bx16_0_63, itok_B_207_1644 = _rec_inputs()

    def _L0_cond_setup():
        import jax, jax.numpy as jnp
        import numpy as np
        B, C, T = (64, 32, 512)
        S, D = (16, 32)
        key = jax.random.key(seed)
        k1, k2, k3 = jax.random.split(key, 3)
        x = jax.random.normal(k1, (B, C, T), dtype=jnp.float32)
        condition = jax.random.randint(k2, (B,), 0, S, dtype=jnp.int64)
        bound = float(np.sqrt(6.0 / C))
        weights = jax.random.uniform(k3, (S, C, D), dtype=jnp.float32, minval=-bound, maxval=bound)
        return {'x': x, 'condition': condition, 'weights': weights}
    _L0_cond_all = _L0_cond_setup()
    _L0_cond_in = {k: v for k, v in _L0_cond_all.items() if k in ('weights',)}
    del _L0_cond_all

    def _L1_cond_setup():
        import jax, jax.numpy as jnp
        import numpy as np
        B, S, D_IN, D_OUT = (4, 256, 512, 512)
        RANK, MAX_LORAS = (16, 32)
        key = jax.random.key(seed)
        ks = jax.random.split(key, 6)
        x = jax.random.normal(ks[0], (B, S, D_IN), dtype=jnp.float32)
        adapter_ids = jax.random.randint(ks[1], (B,), 0, MAX_LORAS)
        base_weight = jax.random.normal(ks[2], (D_OUT, D_IN), dtype=jnp.float32) * D_IN ** (-0.5)
        base_bias = jax.random.normal(ks[3], (D_OUT,), dtype=jnp.float32) * 0.01
        lora_A_w = jax.random.normal(ks[4], (MAX_LORAS, RANK, D_IN), dtype=jnp.float32) * D_IN ** (-0.5)
        lora_B_w = jax.random.normal(ks[5], (MAX_LORAS, D_OUT, RANK), dtype=jnp.float32) * RANK ** (-0.5)
        return {'x': x, 'adapter_ids': adapter_ids, 'base_weight': base_weight, 'base_bias': base_bias, 'lora_A_w': lora_A_w, 'lora_B_w': lora_B_w}
    _L1_cond_all = _L1_cond_setup()
    _L1_cond_in = {k: v for k, v in _L1_cond_all.items() if k in ('base_weight', 'base_bias', 'lora_A_w', 'lora_B_w')}
    del _L1_cond_all

    def _L2_cond_setup():
        import jax, jax.numpy as jnp
        import numpy as np
        B, S, HID = (4, 128, 512)
        D, HQ, HK = (128, 32, 8)
        PAGES, PSIZE, NPP = (64, 32, 16)
        THETA = 10000.0
        EPS = 1e-06
        SCALE = 1.0 / float(np.sqrt(D))

        def _rmsnorm(t, w):
            var = jnp.mean(t * t, axis=-1, keepdims=True)
            return t * jax.lax.rsqrt(var + EPS) * w

        def _rope(t, pos):
            inv_freq = 1.0 / THETA ** (jnp.arange(0, D, 2, dtype=jnp.float32) / D)
            freqs = pos[..., None].astype(jnp.float32) * inv_freq
            cos = jnp.cos(freqs)[:, :, None, :]
            sin = jnp.sin(freqs)[:, :, None, :]
            t1, t2 = (t[..., :D // 2], t[..., D // 2:])
            return jnp.concatenate([t1 * cos - t2 * sin, t2 * cos + t1 * sin], axis=-1)
        key = jax.random.key(seed)
        ks = jax.random.split(key, 10)
        x = jax.random.normal(ks[0], (B, S, HID), jnp.float32)
        Wq = jax.random.normal(ks[1], (HQ * D, HID), jnp.float32) * 0.02
        Wk = jax.random.normal(ks[2], (HK * D, HID), jnp.float32) * 0.02
        Wv = jax.random.normal(ks[3], (HK * D, HID), jnp.float32) * 0.02
        Wo = jax.random.normal(ks[4], (HID, HQ * D), jnp.float32) * 0.02
        q_norm_w = jax.random.uniform(ks[5], (D,), jnp.float32)
        k_norm_w = jax.random.uniform(ks[6], (D,), jnp.float32)
        k_cache = jax.random.normal(ks[7], (PAGES, PSIZE, HK, D), jnp.float32)
        v_cache = jax.random.normal(ks[8], (PAGES, PSIZE, HK, D), jnp.float32)
        block_table = jnp.arange(B * NPP, dtype=jnp.int32).reshape(B, NPP)
        cache_seqlens = jax.random.randint(ks[9], (B,), 0, 475).astype(jnp.int32)
        return dict(x=x, Wq=Wq, Wk=Wk, Wv=Wv, Wo=Wo, q_norm_w=q_norm_w, k_norm_w=k_norm_w, k_cache=k_cache, v_cache=v_cache, block_table=block_table, cache_seqlens=cache_seqlens)
    _L2_cond_all = _L2_cond_setup()
    _L2_cond_in = {k: v for k, v in _L2_cond_all.items() if k in ('Wq', 'Wk', 'Wv', 'Wo', 'q_norm_w', 'k_norm_w', 'k_cache', 'v_cache')}
    del _L2_cond_all

    def _L3_cond_setup():
        import jax, jax.numpy as jnp
        import numpy as np
        NUM_CONDITIONS = 16
        IN_CH = 32
        OUT_CH = 32
        B = 64
        T = 512
        key = jax.random.key(seed)
        k_x, k_w, k_c = jax.random.split(key, 3)
        x = jax.random.normal(k_x, (B, IN_CH, T), dtype=jnp.float32)
        bound = float(np.sqrt(6.0 / IN_CH))
        weights = jax.random.uniform(k_w, (NUM_CONDITIONS, IN_CH, OUT_CH), dtype=jnp.float32, minval=-bound, maxval=bound)
        condition = jax.random.randint(k_c, (B,), 0, NUM_CONDITIONS, dtype=jnp.int64)
        return {'x': x, 'weights': weights, 'condition': condition}
    _L3_cond_all = _L3_cond_setup()
    _L3_cond_in = {k: v for k, v in _L3_cond_all.items() if k in ('weights',)}
    del _L3_cond_all
    return {'x': x, 'itok_B_0_15': itok_B_0_15, 'itok_B_6_15': itok_B_6_15, 'itok_Bx16_0_63': itok_Bx16_0_63, 'itok_B_207_1644': itok_B_207_1644, 'L0_cond_weights': _L0_cond_in['weights'], 'L1_cond_base_weight': _L1_cond_in['base_weight'], 'L1_cond_base_bias': _L1_cond_in['base_bias'], 'L1_cond_lora_A_w': _L1_cond_in['lora_A_w'], 'L1_cond_lora_B_w': _L1_cond_in['lora_B_w'], 'L2_cond_Wq': _L2_cond_in['Wq'], 'L2_cond_Wk': _L2_cond_in['Wk'], 'L2_cond_Wv': _L2_cond_in['Wv'], 'L2_cond_Wo': _L2_cond_in['Wo'], 'L2_cond_q_norm_w': _L2_cond_in['q_norm_w'], 'L2_cond_k_norm_w': _L2_cond_in['k_norm_w'], 'L2_cond_k_cache': _L2_cond_in['k_cache'], 'L2_cond_v_cache': _L2_cond_in['v_cache'], 'L3_cond_weights': _L3_cond_in['weights']}

def reference(x, itok_B_0_15, itok_B_6_15, itok_Bx16_0_63, itok_B_207_1644, L0_cond_weights, L1_cond_base_weight, L1_cond_base_bias, L1_cond_lora_A_w, L1_cond_lora_B_w, L2_cond_Wq, L2_cond_Wk, L2_cond_Wv, L2_cond_Wo, L2_cond_q_norm_w, L2_cond_k_norm_w, L2_cond_k_cache, L2_cond_v_cache, L3_cond_weights):
    import jax
    import jax.numpy as jnp

    def _L0_cond_ref(x, condition, weights):
        import jax, jax.numpy as jnp
        import numpy as np
        B, C, T = (64, 32, 512)
        S, D = (16, 32)
        W = weights[condition]
        return jnp.einsum('bct,bcd->bdt', x, W)

    def _L1_cond_ref(x, adapter_ids, base_weight, base_bias, lora_A_w, lora_B_w):
        import jax, jax.numpy as jnp
        import numpy as np
        B, S, D_IN, D_OUT = (4, 256, 512, 512)
        RANK, MAX_LORAS = (16, 32)
        result = jnp.einsum('bsd,od->bso', x, base_weight) + base_bias
        A = lora_A_w[adapter_ids]
        Bw = lora_B_w[adapter_ids]
        h = jnp.einsum('bsd,brd->bsr', x, A)
        lora_out = jnp.einsum('bsr,bor->bso', h, Bw)
        result = result + lora_out
        return result.astype(x.dtype)

    def _L2_cond_ref(x, Wq, Wk, Wv, Wo, q_norm_w, k_norm_w, k_cache, v_cache, block_table, cache_seqlens):
        import jax, jax.numpy as jnp
        import numpy as np
        B, S, HID = (4, 128, 512)
        D, HQ, HK = (128, 32, 8)
        PAGES, PSIZE, NPP = (64, 32, 16)
        THETA = 10000.0
        EPS = 1e-06
        SCALE = 1.0 / float(np.sqrt(D))

        def _rmsnorm(t, w):
            var = jnp.mean(t * t, axis=-1, keepdims=True)
            return t * jax.lax.rsqrt(var + EPS) * w

        def _rope(t, pos):
            inv_freq = 1.0 / THETA ** (jnp.arange(0, D, 2, dtype=jnp.float32) / D)
            freqs = pos[..., None].astype(jnp.float32) * inv_freq
            cos = jnp.cos(freqs)[:, :, None, :]
            sin = jnp.sin(freqs)[:, :, None, :]
            t1, t2 = (t[..., :D // 2], t[..., D // 2:])
            return jnp.concatenate([t1 * cos - t2 * sin, t2 * cos + t1 * sin], axis=-1)
        bsz, seqlen, _ = x.shape
        q = jnp.einsum('bsd,ed->bse', x, Wq).reshape(bsz, seqlen, HQ, D)
        k = jnp.einsum('bsd,ed->bse', x, Wk).reshape(bsz, seqlen, HK, D)
        v = jnp.einsum('bsd,ed->bse', x, Wv).reshape(bsz, seqlen, HK, D)
        q = _rmsnorm(q, q_norm_w)
        k = _rmsnorm(k, k_norm_w)
        pos = cache_seqlens[:, None] + jnp.arange(seqlen)[None, :]
        q = _rope(q, pos)
        k = _rope(k, pos)
        L = NPP * PSIZE
        kc = k_cache[block_table].reshape(bsz, L, HK, D)
        vc = v_cache[block_table].reshape(bsz, L, HK, D)
        k_all = jnp.concatenate([kc, k], axis=1)
        v_all = jnp.concatenate([vc, v], axis=1)
        valid_c = jnp.arange(L)[None, :] < cache_seqlens[:, None]
        valid = jnp.concatenate([valid_c, jnp.ones((bsz, seqlen), dtype=bool)], axis=1)
        rep = HQ // HK
        k_all = jnp.repeat(k_all, rep, axis=2)
        v_all = jnp.repeat(v_all, rep, axis=2)
        scores = jnp.einsum('bqhd,bkhd->bhqk', q, k_all) * SCALE
        scores = jnp.where(valid[:, None, None, :], scores, -1e+30)
        probs = jax.nn.softmax(scores, axis=-1)
        o = jnp.einsum('bhqk,bkhd->bqhd', probs, v_all)
        o = o.reshape(bsz, seqlen, HQ * D)
        return jnp.einsum('bse,de->bsd', o, Wo)

    def _L3_cond_ref(x, weights, condition):
        import jax, jax.numpy as jnp
        import numpy as np
        NUM_CONDITIONS = 16
        IN_CH = 32
        OUT_CH = 32
        B = 64
        T = 512
        W = weights[condition]
        return jnp.einsum('bct,bcd->bdt', x, W)
    x = x + _L0_cond_ref(x, itok_B_0_15, L0_cond_weights)
    x = x + _L1_cond_ref(x, itok_B_6_15, L1_cond_base_weight, L1_cond_base_bias, L1_cond_lora_A_w, L1_cond_lora_B_w)
    x = x + _L2_cond_ref(x, L2_cond_Wq, L2_cond_Wk, L2_cond_Wv, L2_cond_Wo, L2_cond_q_norm_w, L2_cond_k_norm_w, L2_cond_k_cache, L2_cond_v_cache, itok_Bx16_0_63, itok_B_207_1644)
    x = x + _L3_cond_ref(x, L3_cond_weights, itok_B_0_15)
    return x

_drawn_inputs = setup_inputs


def setup_inputs(seed=0):
    import zlib

    import numpy as np

    out = dict(_drawn_inputs(seed))
    spreads = {}
    factors = {'L1_cond_base_bias': 8.0,
     'L2_cond_Wq': 4.15,
     'L2_cond_Wk': 8.0,
     'L2_cond_Wv': 8.0,
     'L2_cond_q_norm_w': 7.211,
     'L2_cond_k_norm_w': 8.0,
     'L2_cond_k_cache': 4.24}
    for name, (base, spread) in spreads.items():
        noise = np.random.default_rng([zlib.crc32(name.encode()), seed]).standard_normal(out[name].shape)
        drawn = base * np.exp(spread * noise) if base else spread * noise
        out[name] = jnp.asarray(drawn.astype(out[name].dtype))
    for name, factor in factors.items():
        out[name] = (out[name] * factor).astype(out[name].dtype)
    return out
```

```python
from contextlib import ExitStack

import concourse.bass as bass
import numpy as np
from concourse import mybir

F32 = mybir.dt.float32
I32 = mybir.dt.int32
ALU = mybir.AluOpType
ACT = mybir.ActivationFunctionType

B, C, T = 64, 32, 512
D, HQ, HK = 128, 32, 8
REP = HQ // HK
PAGES, PSIZE, NPP = 64, 32, 16
L = NPP * PSIZE
RANK, LORAS = 16, 32
CONDS = 16
P = 128
BT = P // C
NT = B // BT
HC = T // P
KW = (NPP + 1) * PSIZE
PW = 5 * P
QKB = HQ // 4 + HK // 4
VB = HK // 4
UG = BT * HK
NU = B * HK
LAG = 3
ROT = 9
WO_HEADS = [0, 5, 5, 5, 5, 5, 5, 2]

SCALE = 1.0 / float(np.sqrt(D))
EPS = 1e-6
NEG = -1e30
TWO_PI = 2.0 * np.pi
C1 = 6.28125
C2 = float(np.float32(1.93500518798828125e-3))
C3 = float(np.float32(TWO_PI - 6.28125 - 1.93500518798828125e-3))
ROUND = 1.5 * 2.0 ** 23
PI_IN = float(np.nextafter(np.float32(np.pi), np.float32(0)))


def ge(eng, sem, val):
    if not isinstance(val, int) or val > 0:
        eng.wait_ge(sem, val)


def build(nc, x, cond_row, id_row, bt_row, idx_pages, seq_tok, seq_all, w0, w3, wb, bias,
          lora_a, lora_b, wqk, wv, wo, qn, kn, kT_cache, v_cache, ident_c, iota_c, row_c, invf_c,
          hmask_c, out):
    ctx = ExitStack()
    with ctx:
        def sb(name, shape, dt=F32):
            return ctx.enter_context(nc.sbuf_tensor(name, shape, dt))

        def sem(name):
            return ctx.enter_context(nc.semaphore(name))

        qkT_d = nc.dram_tensor("qkT_d", (B, D, QKB, P), F32, kind="Internal").ap()
        v_d = nc.dram_tensor("v_d", (NT * P, HK * D), F32, kind="Internal").ap()
        x2_d = nc.dram_tensor("x2_d", (NT, P, T), F32, kind="Internal").ap()

        regA = sb("regA", [P, HQ * T])
        x2T = regA[:, 0:HC * NT * P].rearrange("p (c n) -> p c n", c=HC)
        tabs = regA[:, HC * NT * P:].rearrange("p (k t d) -> p k t d", k=4, t=NT)
        wo_sb = regA[:, :].rearrange("p (h n) -> p h n", h=HQ)
        KSZ, VSZ = (NPP + 1) * HK * PSIZE, 5 * HK * D
        regK = sb("regK", [P, 2 * KSZ + 2 * VSZ])
        k_sb = [regK[:, i * KSZ:(i + 1) * KSZ].rearrange("p (s h t) -> p s h t", s=NPP + 1, h=HK) for i in range(2)]
        v_sb = [regK[:, 2 * KSZ + i * VSZ:2 * KSZ + (i + 1) * VSZ].rearrange("p (k n) -> p k n", k=5) for i in range(2)]
        at = [0]

        def inK(n):
            at[0] += n
            assert at[0] <= 2 * KSZ + 2 * VSZ
            return regK[:, at[0] - n:at[0]]

        wb_sb = inK(HC * T).rearrange("p (c n) -> p c n", c=HC)
        x_sb = [inK(T) for _ in range(4)]
        x1_sb = [inK(T) for _ in range(4)]
        x1T_sb = [inK(T) for _ in range(4)]
        x2_sb = [inK(T) for _ in range(4)]
        bd0 = [inK(P) for _ in range(4)]
        a4 = [inK(BT * HC * RANK).rearrange("p (c n) -> p c n", c=HC) for _ in range(4)]
        b4 = [inK(T) for _ in range(4)]
        hT = [inK(P) for _ in range(4)]
        w0_sb = inK(CONDS * C).rearrange("p (k d) -> p k d", k=CONDS)
        la_sb = inK(LORAS * HC * RANK).rearrange("p (k n) -> p k n", k=LORAS)
        regC = sb("regC", [P, 9728])
        at[0] = 0

        def inC(n):
            at[0] += n
            assert at[0] <= 9728
            return regC[:, at[0] - n:at[0]]

        w_sb = inC(2 * HC * T).rearrange("p (k c n) -> p k c n", k=2, c=HC)
        t1_sb = [inC(T).rearrange("p (h d) -> p h d", h=4) for _ in range(2)]
        t2_sb = [inC(T).rearrange("p (h d) -> p h d", h=4) for _ in range(2)]
        qr_sb = [inC(T) for _ in range(4)]
        st_sb = [inC(T) for _ in range(2)]
        sq_sb = inC(T)
        at[0] = 0
        oT = inC(HQ * P).rearrange("p (h n) -> p h n", h=HQ)
        p_sb = [inC(PW) for _ in range(4)]
        pT_sb = [inC(PW) for _ in range(2)]
        x2r = inC(T)
        x3_sb = inC(T)
        o_sb = inC(T)
        q_sb = [sb(f"q_sb{i}", [P, HK * P]) for i in range(2)]
        mask = [sb(f"mask{i}", [P, KW]) for i in range(2)]
        ident = sb("ident", [P, P])
        iota = sb("iota", [P, L])
        rowc = sb("rowc", [P, 1])
        hmask = sb("hmask", [BT * RANK, P])
        seqt = sb("seqt", [P, NT], I32)
        pos = sb("pos", [P, NT])
        seqi = sb("seqi", [P, B], I32)
        seqf = sb("seqf", [P, B])
        invf = sb("invf", [P, D // 2])
        qn_sb = sb("qn_sb", [P, 2, D])
        HD = D // 2
        ang, turns, red = (regA[:, HC * NT * P + 4096 + i * NT * HD:HC * NT * P + 4096 + (i + 1) * NT * HD] for i in range(3))
        trig = [q_sb[i][:, 0:NT * HD] for i in range(2)]
        idxi = sb("idxi", [P, B * 4], I32)
        idx_all = sb("idx_all", [P, B * 4], I32)
        idx = [sb(f"idx{i}", [P, 4], I32) for i in range(4)]
        cond = sb("cond", [1, B], I32)
        ids = sb("ids", [1, B], I32)
        btab = sb("btab", [1, B * NPP], I32)
        w3_sb = sb("w3_sb", [P, CONDS, C])
        bd3 = sb("bd3", [P, P])
        ss = sb("ss", [P, 4, 4])
        sd = sb("sd", [P, 4, 4])
        rstd = sb("rstd", [P, 4, 4])
        epsc = sb("epsc", [P, 1])
        nmx = sb("nmx", [P, 4])
        rs = sb("rs", [P, 4])
        rinv = sb("rinv", [P, 4])
        hold = sb("hold", [P, 4])

        S = [ctx.enter_context(nc.psum_tensor(f"S{i}", [P, 1024], F32)) for i in range(2)]
        bank4 = [ctx.enter_context(nc.psum_tensor(f"bank{i}", [P, 512], F32)) for i in range(4, 8)]
        bank = [S[0][:, 0:512], S[0][:, 512:1024], S[1][:, 0:512], S[1][:, 512:1024]] + [b[:, :] for b in bank4]
        pTA, pTB, oP, yP = bank[4:8]
        S0 = 512 - 9 * PSIZE
        scores = [S[i][:, S0:S0 + KW] for i in range(2)]

        s_small, s_rope_in = sem("s_small"), sem("s_rope_in")
        s_wts = sem("s_wts")
        s_xin = [sem(f"s_xin{j}") for j in range(4)]
        s_ones, s_zero = sem("s_ones"), sem("s_zero")
        s_pick = [sem(f"s_pick{j}") for j in range(4)]
        s_pick0 = [sem(f"s_pick0{j}") for j in range(4)]
        s_mm0, s_x1, s_tx1, s_x1T = sem("s_mm0"), sem("s_x1"), sem("s_tx1"), sem("s_x1T")
        s_hmm, s_hT, s_mm1, s_x2 = sem("s_hmm"), sem("s_hT"), sem("s_mm1"), sem("s_x2")
        s_tx2, s_x2T = sem("s_tx2"), sem("s_x2T")
        s_x2st = [sem(f"s_x2st{j}") for j in range(4)]
        s_ang, s_sin, s_tab, s_dve = sem("s_ang"), sem("s_sin"), sem("s_tab"), sem("s_dve")
        s_vz, s_pad, s_idx0 = sem("s_vz"), sem("s_pad"), sem("s_idx0")
        s_w = sem("s_w")
        s_vp, s_vc = sem("s_vp"), sem("s_vc")
        s_vst = [sem(f"s_vst{i}") for i in range(2)]
        s_pj, s_ss, s_sd, s_rstd = sem("s_pj"), sem("s_ss"), sem("s_sd"), sem("s_rstd")
        s_rot, s_qr, s_tq, s_qT = sem("s_rot"), sem("s_qr"), sem("s_tq"), sem("s_qT")
        s_qst = [sem(f"s_qst{i}") for i in range(2)]
        s_wo_in, s_idx = sem("s_wo_in"), sem("s_idx")
        s_k = [sem(f"s_k{i}") for i in range(2)]
        s_v = [sem(f"s_v{i}") for i in range(2)]
        s_vs = [sem(f"s_vs{i}") for i in range(2)]
        s_mask, s_qk, s_mx, s_exp = sem("s_mask"), sem("s_qk"), sem("s_mx"), sem("s_exp")
        s_ri, s_p, s_ta, s_tb = sem("s_ri"), sem("s_p"), sem("s_ta"), sem("s_tb")
        s_evA, s_evB, s_pv, s_oev = sem("s_evA"), sem("s_evB"), sem("s_pv"), sem("s_oev")
        s_wo, s_x3, s_bd3, s_l3 = sem("s_wo"), sem("s_x3"), sem("s_bd3"), sem("s_l3")
        s_out, s_outst, s_x2r = sem("s_out"), sem("s_outst"), sem("s_x2r")
        SMALL = 16 * 8
        WTS = 16 * 4
        KLOAD = 16 * (NPP + 2)
        block = ctx.enter_context(nc.Block())

        @block.sync
        def _(sp):
            SP = [mybir.EngineType.SP]
            for dst, src in ((seqt, seq_tok), (invf, invf_c), (rowc, row_c), (qn_sb[:, 0, :], qn), (qn_sb[:, 1, :], kn)):
                sp.dma_start(dst[:], src).then_inc(s_rope_in, 16)
            for dst, src in ((cond, cond_row), (ids, id_row), (btab, bt_row), (ident, ident_c), (hmask, hmask_c),
                             (iota, iota_c), (seqi, seq_all), (idxi, idx_pages)):
                sp.dma_start(dst[:], src).then_inc(s_small, 16)
            for dst, src in ((w0_sb, w0), (w3_sb[:], w3), (la_sb, lora_a), (wb_sb, wb)):
                sp.dma_start(dst, src).then_inc(s_wts, 16)
            for j in range(4):
                sp.dma_start(b4[j][BT * RANK:BT * RANK + 1, :], bias).then_inc(s_wts, 16)
            sp.wait_ge(s_small, SMALL)

            def load_tile(i, j):
                sp.dma_start(x_sb[j], x[bass.ds(i * 4 + j, 1)].rearrange("a p n -> p (a n)")).then_inc(s_xin[j], 16)
                _, rows = nc.values_load_multi_w_load_instructions(
                    ids[0:1, bass.ds(i * 16 + 4 * j, BT)], engines=SP, min_val=0, max_val=LORAS - 1)
                for b in range(BT):
                    sp.dma_start(b4[j][b * RANK:(b + 1) * RANK, :],
                                 lora_b[bass.ds(rows[b], 1)].rearrange("a r n -> r (a n)")).then_inc(s_xin[j], 16)

            for j in range(4):
                load_tile(0, j)
            sp.dma_start(w_sb[:, 0, :, :], wv[0]).then_inc(s_w, 16)
            sp.wait_ge(s_w, 16)
            sp.dma_start(w_sb[:, 1, :, :], wv[1]).then_inc(s_w, 16)
            with sp.Fori(1, NT // 4) as i:
                for j in range(4):
                    sp.wait_ge(s_x1, i * 4 - 3 + j)
                    sp.wait_ge(s_mm1, i * 4 - 3 + j)
                    load_tile(i, j)

            for j in range(VB):
                for t in range(NT):
                    sp.wait_ge(s_vc, j * NT + t + 1)
                    sp.dma_start(v_d[t * P:(t + 1) * P, j * T:(j + 1) * T], st_sb[t % 2]).then_inc(s_vst[t % 2], 16)
                sp.wait_ge(s_vp, (j + 1) * NT)
                sp.wait_ge(s_w, 16 * (2 + j))
                sp.dma_start(w_sb[:, j, :, :], wqk[j]).then_inc(s_w, 16)

            def load_pages(b, par):
                _, pages = nc.values_load_multi_w_load_instructions(
                    btab[0:1, bass.ds(b * NPP, NPP)], engines=SP, min_val=0, max_val=PAGES - 1)
                for n in range(NPP):
                    sp.dma_start(k_sb[par][:, n, :, :].rearrange("p h t -> p (h t)"),
                                 kT_cache[bass.ds(pages[n], 1)].rearrange("a p n -> p (a n)")).then_inc(s_k[par], 16)

            def load_own(b, par):
                sp.dma_start(k_sb[par][:, NPP, :, :].rearrange("p h t -> p (h t)"),
                             qkT_d[bass.ds(b, 1), :, HK:QKB, :].rearrange("a p e n -> p (a e n)")).then_inc(s_k[par], 16)
                sp.dma_start(q_sb[par][:, :],
                             qkT_d[bass.ds(b, 1), :, 0:HK, :].rearrange("a p e n -> p (a e n)")).then_inc(s_k[par], 16)

            def load_own_v(b, par):
                sp.dma_start(v_sb[par][0:C, 4, :], v_d[bass.ds(b * C, C), :]).then_inc(s_vs[par], 16)

            sp.wait_ge(s_x2T, NT)
            for j in range(4):
                sp.wait_ge(s_x2st[j], 16 * (NT // 4))
            for b in range(2):
                load_pages(b, b)

            def store_qk(e, t):
                sp.wait_ge(s_qT, e * NT + t + 1)
                sp.dma_start(qkT_d[t * BT:(t + 1) * BT, :, bass.ds(e, 1), :].rearrange("b p a n -> p b (a n)"),
                             st_sb[t % 2].rearrange("p (b n) -> p b n", b=BT)).then_inc(s_qst[t % 2], 16)

            with sp.Fori(0, (QKB - 2) // 2) as ee:
                for k in range(2):
                    e = ee * 2 + k
                    for t in range(NT):
                        store_qk(e, t)
                        if t == NT - LAG:
                            sp.dma_start(w_sb[:, k, :, :].rearrange("p c n -> p (c n)"),
                                         wqk[bass.ds(e + 2, 1)].rearrange("a p c n -> p (a c n)")).then_inc(s_w, 16)
            with sp.Fori(QKB - 2, QKB) as e:
                for t in range(NT):
                    store_qk(e, t)

            for j in range(2):
                sp.wait_ge(s_qst[j], 16 * QKB * NT // 2)
                sp.wait_ge(s_vst[j], 16 * VB * NT // 2)
            sp.wait_ge(s_vz, 2)
            for b in range(2):
                load_own(b, b)
                load_own_v(b, b)
            for h in range(4):
                sp.dma_start(wo_sb[:, h * 8:(h + 1) * 8, :], wo[:, h * 8:(h + 1) * 8, :]).then_inc(s_wo_in, 16)

            def group(g, first, last):
                for k in range(2 if last else 4):
                    b = g * 4 + (k + 2)
                    par = k % 2
                    sp.wait_ge(s_qk, g * UG + HK * (k + 1))
                    load_pages(b, par)
                    load_own(b, par)
                    sp.wait_ge(s_pv, g * UG + HK * (k + 1))
                    load_own_v(b, par)
                    if k == 1 and not first:
                        sp.wait_ge(s_out, g)
                        sp.dma_start(out[bass.ds(g - 1, 1)].rearrange("a p n -> p (a n)"), o_sb).then_inc(s_outst, 16)
                ge(sp, s_outst, g * 16)
                sp.dma_start(x2r, x2_d[bass.ds(g, 1)].rearrange("a p n -> p (a n)")).then_inc(s_x2r, 16)

            group(0, True, False)
            with sp.Fori(1, NT - 1) as g:
                group(g, False, False)
            group(NT - 1, False, True)
            sp.wait_ge(s_out, NT)
            sp.dma_start(out[NT - 1], o_sb).then_inc(s_outst, 16)
            sp.wait_ge(s_outst, 16 * NT)

        @block.gpsimd
        def _(pool):
            PL = [mybir.EngineType.Pool]
            pool.wait_ge(s_small, SMALL)
            pool.wait_ge(s_wts, 2 * WTS)

            def pick(i, j):
                ge(pool, s_hmm, i * 4 - 3 + j)
                _, rows = nc.values_load_multi_w_load_instructions(
                    ids[0:1, bass.ds(i * 16 + 4 * j, BT)], engines=PL, min_val=0, max_val=LORAS - 1)
                for b in range(BT):
                    nc.gpsimd.tensor_copy(a4[j][:, :, b * RANK:(b + 1) * RANK],
                                          la_sb[:, bass.ds(rows[b], 1), :].rearrange("p a (c r) -> p (a c) r", c=HC))\
                        .then_inc(s_pick[j], 1)

            for j in range(4):
                pick(0, j)
            with pool.Fori(1, NT // 4) as i:
                for j in range(4):
                    pick(i, j)

            pool.wait_ge(s_x2T, NT)
            for j in range(4):
                pool.wait_ge(s_x2st[j], 16 * (NT // 4))
            for i in range(2):
                nc.gpsimd.memset(v_sb[i][:, 4, :], 0.0).then_inc(s_vz, 1)

            def next_idx(b, k):
                nc.gpsimd.tensor_copy(idx[k][:], idx_all[:, bass.ds(b * 4, 4)]).then_inc(s_idx, 1)

            def gather_v(k, par):
                for m in range(4):
                    nc.gpsimd.indirect_dma_start(
                        out=v_sb[par][:, m, :], out_offset=None, in_=v_cache,
                        in_offset=bass.IndirectOffsetOnAxis(ap=idx[k][:, m:m + 1], axis=0)).then_inc(s_v[par], 16)

            pool.wait_ge(s_idx0, 1)
            next_idx(0, 0)
            next_idx(1, 1)
            next_idx(2, 2)
            pool.wait_ge(s_idx, 2)
            gather_v(0, 0)
            gather_v(1, 1)

            def add_halves(e, t):
                pool.wait_ge(s_rot, e * NT + t + 1)
                ge(pool, s_tq, e * NT + t - 3)
                qv = qr_sb[t % 4].rearrange("p (h d) -> p h d", h=4)
                for lo, hi in ((0, HD), (HD, 0)):
                    nc.gpsimd.tensor_tensor(qv[:, :, lo:lo + HD], t1_sb[t % 2][:, :, lo:lo + HD],
                                            t2_sb[t % 2][:, :, hi:hi + HD], ALU.add).then_inc(s_qr, 1)

            for t in range(NT):
                add_halves(0, t)
            with pool.Fori(1, QKB) as e:
                for t in range(NT):
                    add_halves(e, t)

            pool.wait_ge(s_tq, QKB * NT)
            for i in range(4):
                nc.gpsimd.memset(p_sb[i][:, KW:PW], 0.0).then_inc(s_pad, 1)

            def group(g, last):
                for k in range(2 if last else 4):
                    b = g * 4 + (k + 2)
                    pool.wait_ge(s_idx, b + 1)
                    pool.wait_ge(s_pv, g * UG + HK * (k + 1))
                    if not (last and k == 1):
                        next_idx(b + 1, (k + 3) % 4)
                    gather_v((k + 2) % 4, k % 2)

            group(0, False)
            with pool.Fori(1, NT - 1) as g:
                group(g, False)
            group(NT - 1, True)

        @block.scalar
        def _(act):
            def pick(dst, table, tile, done):
                _, cs = nc.values_load_multi_w_load_instructions(
                    cond[0:1, bass.ds(tile * BT, BT)], engines=[mybir.EngineType.Activation], min_val=0, max_val=CONDS - 1)
                for b in range(BT):
                    at = slice(b * C, (b + 1) * C)
                    nc.scalar.copy(dst[at, at], table[at, bass.ds(cs[b], 1), :].rearrange("p a d -> p (a d)")).then_inc(done, 1)

            def tile1a(i, last):
                for j in range(4):
                    act.wait_ge(s_tx1, i * 4 + j + 1)
                    nc.scalar.copy(x1T_sb[j], bank[4 + j]).then_inc(s_x1T, 1)
                    if not last:
                        pick(bd0[j], w0_sb, i * 4 + (4 + j), s_pick0[j])
                for j in range(4):
                    act.wait_ge(s_tx2, i * 4 + j + 1)
                    nc.scalar.copy(x2T[:, :, bass.ds((i * 4 + j) * P, P)],
                                   bank[4 + j].rearrange("p (c n) -> p c n", c=HC)).then_inc(s_x2T, 1)
                    act.dma_start(x2_d[bass.ds(i * 4 + j, 1)].rearrange("a p n -> p (a n)"), x2_sb[j]).then_inc(s_x2st[j], 16)

            act.wait_ge(s_small, SMALL)
            act.wait_ge(s_wts, 2 * WTS)
            act.wait_ge(s_zero, 5)
            for j in range(4):
                pick(bd0[j], w0_sb, j, s_pick0[j])
            with act.Fori(0, NT // 4 - 1) as i:
                tile1a(i, False)
            tile1a(NT // 4 - 1, True)

            for j in range(VB):
                for t in range(NT):
                    u = j * NT + t
                    act.wait_ge(s_vp, u + 1)
                    ge(act, s_vst[t % 2], 16 * (u // 2))
                    nc.scalar.copy(st_sb[t % 2], bank[t % 4]).then_inc(s_vc, 1)
                if j == 0:
                    for k in range(2):
                        act.wait_ge(s_ang, k + 1)
                        nc.scalar.activation(trig[k], trig[k], ACT.Sin).then_inc(s_sin, 1)

            def squares(e, t):
                act.wait_ge(s_pj, e * NT + t + 1)
                for h in range(4):
                    last = nc.scalar.activation(sq_sb[:, h * D:(h + 1) * D], bank[t % 4][:, h * D:(h + 1) * D], ACT.Square,
                                                accum_out=ss[:, t % 4, h:h + 1])
                last.then_inc(s_ss, 1)
                act.wait_ge(s_ss, e * NT + t + 1)
                nc.scalar.activation(sd[:, t % 4, :], ss[:, t % 4, :], ACT.Sqrt, bias=epsc[:], scale=1.0 / D).then_inc(s_sd, 1)

            def evac(e, t):
                act.wait_ge(s_tq, e * NT + t + 1)
                ge(act, s_qst[t % 2], e * 128 + 16 * (t // 2))
                nc.scalar.copy(st_sb[t % 2].rearrange("p (b h s) -> p h b s", b=BT, h=4),
                               bank[4 + t % 2].rearrange("p (h b s) -> p h b s", h=4, b=BT)).then_inc(s_qT, 1)

            def ahead(e, t):
                return (e, t + LAG) if t + LAG < NT else (e + 1, t + LAG - NT)

            for j in range(2):
                act.wait_ge(s_vst[j], 16 * VB * NT // 2)
            act.wait_ge(s_tab, 1)
            for t in range(LAG):
                squares(0, t)
            for t in range(NT):
                squares(*ahead(0, t))
                evac(0, t)
            with act.Fori(1, QKB - 1) as e:
                for t in range(NT):
                    squares(*ahead(e, t))
                    evac(e, t)
            for t in range(NT):
                if t + LAG < NT:
                    squares(QKB - 1, t + LAG)
                evac(QKB - 1, t)

            def exps(n, u):
                act.wait_ge(s_mx, n + 1)
                nc.scalar.activation(p_sb[u % 4][:, 0:KW], p_sb[u % 4][:, 0:KW], ACT.Exp, bias=nmx[:, u % 4:u % 4 + 1],
                                     scale=-1.0, accum_out=rs[:, u % 4:u % 4 + 1]).then_inc(s_exp, 1)

            def out_head(n, u):
                act.wait_ge(s_pv, n + 1)
                b, h = u // HK % BT, u % HK
                nc.scalar.copy(oT[:, h * REP:(h + 1) * REP, b * C:(b + 1) * C],
                               oP[:, 0:P].rearrange("p (r s) -> p r s", r=REP)).then_inc(s_oev, 1)

            def step(g, u):
                n = g * UG + u
                act.wait_ge(s_ta, n + 1)
                ge(act, s_pv, n - 1)
                nc.scalar.copy(pT_sb[u % 2][:, 0:4 * P], pTA).then_inc(s_evA, 1)
                if not (isinstance(n, int) and n + 2 >= NU):
                    exps(n + 2, u + 2)
                if not (isinstance(n, int) and n == 0):
                    out_head(n - 1, (u - 1) % UG)
                if u == ROT + 1:
                    pick(bd3, w3_sb, g, s_bd3)

            exps(0, 0)
            exps(1, 1)
            for u in range(ROT):
                step(0, u)
            with act.Fori(0, NT - 1) as g:
                for u in range(ROT, UG):
                    step(g, u)
                for u in range(ROT):
                    step(g + 1, u)
            for u in range(ROT, UG):
                step(NT - 1, u)
            out_head(NU - 1, UG - 1)

        @block.vector
        def _(dve):
            chain = [0]

            def link(ins):
                chain[0] += 1
                ins.then_inc(s_dve, 1)
                dve.wait_ge(s_dve, chain[0])

            def tile1a(i):
                for j in range(4):
                    dve.wait_ge(s_mm0, i * 4 + j + 1)
                    nc.vector.tensor_tensor(x1_sb[j], bank[j], x_sb[j], ALU.add).then_inc(s_x1, 1)
                for j in range(4):
                    dve.wait_ge(s_hmm, i * 4 + j + 1)
                    nc.vector.tensor_tensor(hT[j][0:BT * RANK, :], bank[4 + j][0:BT * RANK, 0:P], hmask[:], ALU.mult)\
                        .then_inc(s_hT, 1)
                for j in range(4):
                    dve.wait_ge(s_mm1, i * 4 + j + 1)
                    ge(dve, s_tx2, i * 4 - 3 + j)
                    ge(dve, s_x2st[j], i * 16)
                    nc.vector.tensor_tensor(x2_sb[j], bank[j], x1_sb[j], ALU.add).then_inc(s_x2, 1)

            for j in range(4):
                nc.vector.memset(bd0[j], 0.0).then_inc(s_zero, 1)
                nc.vector.memset(hT[j][BT * RANK:BT * RANK + 1, :], 1.0).then_inc(s_ones, 1)
            nc.vector.memset(bd3[:], 0.0).then_inc(s_zero, 1)
            dve.wait_ge(s_small, SMALL)
            tile1a(0)
            with dve.Fori(1, NT // 4) as i:
                tile1a(i)

            dve.wait_ge(s_rope_in, 16 * 5)
            link(nc.vector.tensor_copy(pos[:], seqt[:]))
            link(nc.vector.tensor_scalar(pos[:], pos[:], rowc[:], None, ALU.add))
            a3 = ang.rearrange("p (t f) -> p t f", t=NT)
            link(nc.vector.tensor_tensor(a3, pos[:, :].unsqueeze(2).to_broadcast([P, NT, HD]),
                                         invf[:, :].unsqueeze(1).to_broadcast([P, NT, HD]), ALU.mult))
            for k, turn in ((0, 0.0), (1, 0.25)):
                link(nc.vector.tensor_scalar(red, ang, 1.0 / TWO_PI, turn, ALU.mult, ALU.add))
                link(nc.vector.tensor_scalar(turns, red, ROUND, None, ALU.add))
                link(nc.vector.tensor_scalar(turns, turns, ROUND, None, ALU.subtract))
                link(nc.vector.scalar_tensor_tensor(out=red, in0=turns, scalar=-C1, in1=ang, op0=ALU.mult, op1=ALU.add))
                link(nc.vector.scalar_tensor_tensor(out=red, in0=turns, scalar=-C2, in1=red, op0=ALU.mult, op1=ALU.add))
                link(nc.vector.scalar_tensor_tensor(out=red, in0=turns, scalar=-C3, in1=red, op0=ALU.mult, op1=ALU.add))
                link(nc.vector.tensor_scalar(red, red, turn * TWO_PI, PI_IN, ALU.add, ALU.min))
                nc.vector.tensor_scalar(trig[k], red, -PI_IN, None, ALU.max).then_inc(s_ang, 1)
                dve.wait_ge(s_ang, k + 1)
            for i in range(2):
                nc.vector.memset(mask[i][:, L:KW], 0.0)
            nc.vector.tensor_copy(seqf[:], seqi[:])
            nc.vector.tensor_scalar(idx_all[:], idxi[:], float(PSIZE), rowc[:], ALU.mult, ALU.add).then_inc(s_idx0, 1)
            dve.wait_ge(s_sin, 2)
            sin3, cos3 = (trig[k].rearrange("p (t f) -> p t f", t=NT) for k in range(2))
            for k in range(2):
                for half, sign in ((0, 1.0), (HD, -1.0)):
                    w = qn_sb[:, k, half:half + HD].unsqueeze(1).to_broadcast([P, NT, HD])
                    nc.vector.tensor_tensor(tabs[:, 2 * k, :, half:half + HD], cos3, w, ALU.mult)
                    last = nc.vector.scalar_tensor_tensor(out=tabs[:, 2 * k + 1, :, half:half + HD], in0=sin3, scalar=sign,
                                                          in1=w, op0=ALU.mult, op1=ALU.mult)
            link(last)
            nc.vector.memset(epsc[:], EPS).then_inc(s_tab, 1)

            def rotate(e, t, k):
                n = e * NT + t
                dve.wait_ge(s_sd, n + 1)
                nc.vector.reciprocal(rstd[:, t % 4, :], sd[:, t % 4, :]).then_inc(s_rstd, 1)
                ge(dve, s_qr, n * 2 - 2)
                dve.wait_ge(s_rstd, n + 1)
                for m, dst in ((0, t1_sb), (1, t2_sb)):
                    for h in range(4):
                        last = nc.vector.scalar_tensor_tensor(
                            out=dst[t % 2][:, h, :], in0=bank[t % 4][:, h * D:(h + 1) * D], scalar=rstd[:, t % 4, h:h + 1],
                            in1=tabs[:, 2 * k + m, t, :], op0=ALU.mult, op1=ALU.mult)
                last.then_inc(s_rot, 1)

            for t in range(NT):
                rotate(0, t, 0)
            with dve.Fori(1, HK) as e:
                for t in range(NT):
                    rotate(e, t, 0)
            with dve.Fori(HK, QKB) as e:
                for t in range(NT):
                    rotate(e, t, 1)

            def make_mask(b, par):
                nc.vector.tensor_scalar(mask[par][:, 0:L], iota[:], seqf[:, bass.ds(b, 1)], NEG, ALU.is_ge, ALU.mult)\
                    .then_inc(s_mask, 1)

            def masked_max(n, u, b):
                if u % HK == 0:
                    dve.wait_ge(s_mask, b + 1)
                dve.wait_ge(s_qk, n + 1)
                nc.vector.memset(hold[:, u % 4:u % 4 + 1], 0.0)
                nc.vector.tensor_tensor_reduce(
                    out=p_sb[u % 4][:, 0:KW], in0=scores[u % 2], in1=mask[u // HK % 2][:], scale=-SCALE, scalar=3e38,
                    op0=ALU.add, op1=ALU.min, accum_out=nmx[:, u % 4:u % 4 + 1]).then_inc(s_mx, 1)

            def normalise(n, u):
                dve.wait_ge(s_exp, n + 1)
                nc.vector.reciprocal(rinv[:, u % 4:u % 4 + 1], rs[:, u % 4:u % 4 + 1]).then_inc(s_ri, 1)
                dve.wait_ge(s_ri, n + 1)
                nc.vector.tensor_scalar(p_sb[u % 4][:, 0:KW], p_sb[u % 4][:, 0:KW], rinv[:, u % 4:u % 4 + 1], None, ALU.mult)\
                    .then_inc(s_p, 1)

            def residual(g):
                dve.wait_ge(s_wo, g + 1)
                dve.wait_ge(s_x2r, g * 16 + 16)
                nc.vector.tensor_tensor(x3_sb, yP, x2r, ALU.add).then_inc(s_x3, 1)

            def finish(g):
                dve.wait_ge(s_l3, g + 1)
                nc.vector.tensor_tensor(o_sb, yP, x3_sb, ALU.add).then_inc(s_out, 1)

            def step(g, u, before):
                n = g * UG + u
                last = isinstance(n, int)
                if not (last and n + 1 >= NU):
                    normalise(n + 1, u + 1)
                if u % HK == 3 and not (last and n + HK >= NU):
                    make_mask(g * BT + (u // HK + 1), (u // HK + 1) % 2)
                if not (last and n + 2 >= NU):
                    masked_max(n + 2, u + 2, g * BT + (u + 2) // HK)
                dve.wait_ge(s_tb, n + 1)
                ge(dve, s_pv, n - 1)
                nc.vector.tensor_copy(pT_sb[u % 2][:, 4 * P:PW], pTB[:, 0:P]).then_inc(s_evB, 1)
                if before is not None and u == ROT - 2:
                    residual(before)
                if before is not None and u == ROT - 1:
                    finish(before)

            make_mask(0, 0)
            masked_max(0, 0, 0)
            masked_max(1, 1, 0)
            normalise(0, 0)
            for u in range(ROT):
                step(0, u, None)
            with dve.Fori(0, NT - 1) as g:
                for u in range(ROT, UG):
                    step(g, u, None)
                for u in range(ROT):
                    step(g + 1, u, g)
            for u in range(ROT, UG):
                step(NT - 1, u, None)
            residual(NT - 1)
            finish(NT - 1)

        @block.tensor
        def _(pe):
            def transposes(dst, src):
                for c in range(4):
                    last = nc.tensor.transpose(dst[:, c * P:(c + 1) * P], src[:, c * P:(c + 1) * P], ident[:])
                return last

            def tile1a(i):
                for j in range(4):
                    pe.wait_ge(s_pick0[j], i * 4 + 4)
                    pe.wait_ge(s_xin[j], i * 80 + 80)
                    ge(pe, s_x2, i * 4 - 3 + j)
                    nc.tensor.matmul(bank[j], bd0[j], x_sb[j], start=True, stop=True).then_inc(s_mm0, 1)
                for j in range(4):
                    pe.wait_ge(s_x1, i * 4 + j + 1)
                    ge(pe, s_x2T, i * 4 - 3 + j)
                    transposes(bank[4 + j], x1_sb[j]).then_inc(s_tx1, 1)
                for j in range(4):
                    pe.wait_ge(s_x1T, i * 4 + j + 1)
                    pe.wait_ge(s_pick[j], i * 4 + 4)
                    for c in range(HC):
                        last = nc.tensor.matmul(bank[4 + j][0:BT * RANK, 0:P], a4[j][:, c, :],
                                                x1T_sb[j][:, c * P:(c + 1) * P], start=(c == 0), stop=(c == HC - 1))
                    last.then_inc(s_hmm, 1)
                    for c in range(HC):
                        nc.tensor.matmul(bank[j], x1T_sb[j][:, c * P:(c + 1) * P], wb_sb[:, c, :], start=(c == 0), stop=False)
                for j in range(4):
                    pe.wait_ge(s_hT, i * 4 + j + 1)
                    nc.tensor.matmul(bank[j], hT[j][0:BT * RANK + 1, :], b4[j][0:BT * RANK + 1, :], start=False, stop=True)\
                        .then_inc(s_mm1, 1)
                for j in range(4):
                    pe.wait_ge(s_x2, i * 4 + j + 1)
                    transposes(bank[4 + j], x2_sb[j]).then_inc(s_tx2, 1)

            pe.wait_ge(s_small, SMALL)
            pe.wait_ge(s_wts, 2 * WTS)
            pe.wait_ge(s_ones, 4)
            tile1a(0)
            with pe.Fori(1, NT // 4) as i:
                tile1a(i)

            def project(t, k):
                for c in range(HC):
                    last = nc.tensor.matmul(bank[t % 4], x2T[:, c, t * P:(t + 1) * P], w_sb[:, k, c, :],
                                            start=(c == 0), stop=(c == HC - 1))
                return last

            for j in range(VB):
                pe.wait_ge(s_w, 16 * (j + 1))
                for t in range(NT):
                    if j == 0:
                        pe.wait_ge(s_x2T, t + 1)
                    ge(pe, s_vc, j * NT + t - 3)
                    project(t, j).then_inc(s_vp, 1)

            def project_qk(e, t, k):
                if t == 0:
                    pe.wait_ge(s_w, e * 16 + 48)
                ge(pe, s_rot, e * NT + t - 3)
                project(t, k).then_inc(s_pj, 1)

            def turn_qk(e, t):
                pe.wait_ge(s_qr, e * (2 * NT) + 2 * t + 2)
                ge(pe, s_qT, e * NT + t - 1)
                transposes(bank[4 + t % 2], qr_sb[t % 4]).then_inc(s_tq, 1)

            def block_qk(e, k, last):
                for t in range(NT):
                    if t + LAG < NT:
                        project_qk(e, t + LAG, k)
                    elif not last:
                        project_qk(e + 1, t + LAG - NT, 1 - k)
                    turn_qk(e, t)

            pe.wait_ge(s_vc, VB * NT)
            for t in range(LAG):
                project_qk(0, t, 0)
            block_qk(0, 0, False)
            with pe.Fori(0, QKB // 2 - 1) as ee:
                block_qk(ee * 2 + 1, 1, False)
                block_qk(ee * 2 + 2, 0, False)
            block_qk(QKB - 1, 1, True)

            def score(n, u, pair):
                b, h = u // HK % 2, u % HK
                ge(pe, s_mx, n - 1)
                if h == 0:
                    pe.wait_ge(s_k[b], pair * KLOAD + KLOAD)
                q = q_sb[b][:, h * P:(h + 1) * P]
                nc.tensor.matmul(scores[u % 2][:, 0:9 * PSIZE], q, k_sb[b][:, 0:9, h, :], start=True, stop=True)
                nc.tensor.matmul(scores[u % 2][:, 9 * PSIZE:KW], q, k_sb[b][:, 9:NPP + 1, h, :], start=True, stop=True)\
                    .then_inc(s_qk, 1)

            def turn_p(n, u):
                pe.wait_ge(s_p, n + 1)
                ge(pe, s_evA, n)
                transposes(pTA, p_sb[u % 4]).then_inc(s_ta, 1)
                ge(pe, s_evB, n)
                nc.tensor.transpose(pTB[:, 0:P], p_sb[u % 4][:, 4 * P:PW], ident[:]).then_inc(s_tb, 1)

            def values(n, u, pair):
                b, h = u // HK % 2, u % HK
                if h == 0:
                    pe.wait_ge(s_v[b], pair * 64 + 64)
                    pe.wait_ge(s_vs[b], pair * 16 + 16)
                pe.wait_ge(s_evA, n + 1)
                pe.wait_ge(s_evB, n + 1)
                ge(pe, s_oev, n)
                for m in range(5):
                    last = nc.tensor.matmul(oP[:, 0:P], v_sb[b][:, m, h * D:(h + 1) * D], pT_sb[u % 2][:, m * P:(m + 1) * P],
                                            start=(m == 0), stop=(m == 4))
                last.then_inc(s_pv, 1)

            def out_proj(g, h0, h1):
                if h0 == 0:
                    pe.wait_ge(s_oev, g * UG + UG)
                    pe.wait_ge(s_wo_in, 64)
                for h in range(h0, h1):
                    last = nc.tensor.matmul(yP, oT[:, h, :], wo_sb[:, h, :], start=(h == 0), stop=(h == HQ - 1))
                if h1 == HQ:
                    last.then_inc(s_wo, 1)

            def mix3(g):
                pe.wait_ge(s_x3, g + 1)
                pe.wait_ge(s_bd3, g * BT + BT)
                nc.tensor.matmul(yP, bd3[:], x3_sb, start=True, stop=True).then_inc(s_l3, 1)

            def step(g, u, before):
                n = g * UG + u
                fixed = isinstance(n, int)
                if not (fixed and n + 2 >= NU):
                    score(n + 2, u + 2, g * 2 + (u + 2) // (2 * HK))
                turn_p(n, u)
                if before is not None and u < len(WO_HEADS):
                    h0 = sum(WO_HEADS[:u])
                    if WO_HEADS[u]:
                        out_proj(before, h0, h0 + WO_HEADS[u])
                if before is not None and u == ROT - 1:
                    mix3(before)
                if not (fixed and n == 0):
                    m = (u - 1) % UG
                    values(n - 1, m, g * 2 + m // (2 * HK) if u else g * 2 - 1)

            score(0, 0, 0)
            score(1, 1, 0)
            pe.wait_ge(s_pad, 4)
            for u in range(ROT):
                step(0, u, None)
            with pe.Fori(0, NT - 1) as g:
                for u in range(ROT, UG):
                    step(g, u, None)
                for u in range(ROT):
                    step(g + 1, u, g)
            for u in range(ROT, UG):
                step(NT - 1, u, None)
            values(NU - 1, UG - 1, 2 * NT - 1)
            out_proj(NT - 1, 0, HQ)
            mix3(NT - 1)


def kernel(x, itok_B_0_15, itok_B_6_15, itok_Bx16_0_63, itok_B_207_1644, L0_cond_weights, L1_cond_base_weight,
           L1_cond_base_bias, L1_cond_lora_A_w, L1_cond_lora_B_w, L2_cond_Wq, L2_cond_Wk, L2_cond_Wv, L2_cond_Wo,
           L2_cond_q_norm_w, L2_cond_k_norm_w, L2_cond_k_cache, L2_cond_v_cache, L3_cond_weights):
    import concourse.bacc as bacc
    from concourse.bass_utils import run_bass_kernel_spmd

    def blocks(w, n):
        return np.asarray(w).reshape(n, T, HC, P).transpose(0, 3, 2, 1)

    bt = np.asarray(itok_Bx16_0_63)
    seq = np.asarray(itok_B_207_1644)
    of_row = np.arange(P) // C
    lora_a = np.asarray(L1_cond_lora_A_w).reshape(LORAS, RANK, HC, P).transpose(3, 0, 2, 1).reshape(P, LORAS, HC * RANK)
    arrays = {
        "x": np.asarray(x).reshape(NT, P, T),
        "cond_row": np.asarray(itok_B_0_15).reshape(1, B),
        "id_row": np.asarray(itok_B_6_15).reshape(1, B),
        "bt_row": bt.reshape(1, B * NPP),
        "idx_pages": np.repeat(bt.reshape(B, 4, 4).transpose(2, 0, 1).reshape(4, B * 4), PSIZE, axis=0),
        "seq_tok": seq.reshape(NT, BT)[:, of_row].T,
        "seq_all": np.repeat(seq.reshape(1, B), P, axis=0),
        "w0": np.tile(np.asarray(L0_cond_weights).transpose(1, 0, 2), (BT, 1, 1)),
        "w3": np.tile(np.asarray(L3_cond_weights).transpose(1, 0, 2), (BT, 1, 1)),
        "wb": np.asarray(L1_cond_base_weight).reshape(T, HC, P).transpose(2, 1, 0),
        "bias": np.asarray(L1_cond_base_bias).reshape(1, T),
        "lora_a": lora_a,
        "lora_b": np.asarray(L1_cond_lora_B_w).transpose(0, 2, 1),
        "wqk": np.concatenate([blocks(L2_cond_Wq, HK), blocks(L2_cond_Wk, HK // 4)]),
        "wv": blocks(L2_cond_Wv, VB),
        "wo": np.asarray(L2_cond_Wo).reshape(T, HQ, D).transpose(2, 1, 0),
        "qn": np.repeat(np.asarray(L2_cond_q_norm_w).reshape(1, D), P, axis=0),
        "kn": np.repeat(np.asarray(L2_cond_k_norm_w).reshape(1, D), P, axis=0),
        "kT_cache": np.asarray(L2_cond_k_cache).transpose(0, 3, 2, 1).reshape(PAGES, D, HK * PSIZE),
        "v_cache": np.asarray(L2_cond_v_cache).reshape(PAGES * PSIZE, HK * D),
        "ident_c": np.eye(P, dtype=np.float32),
        "iota_c": np.tile(np.arange(L, dtype=np.float32), (P, 1)),
        "row_c": (np.arange(P) % C).astype(np.float32).reshape(P, 1),
        "invf_c": np.tile((1.0 / 10000.0 ** (np.arange(0, D, 2) / D)).astype(np.float32), (P, 1)),
        "hmask_c": np.repeat(np.repeat(np.eye(BT, dtype=np.float32), RANK, axis=0), C, axis=1),
    }
    arrays = {k: np.ascontiguousarray(v) for k, v in arrays.items()}
    nc = bacc.Bacc("TRN2", target_bir_lowering=False, num_devices=1)
    aps = {k: nc.dram_tensor(k, v.shape, mybir.dt.from_np(v.dtype), kind="ExternalInput").ap() for k, v in arrays.items()}
    aps["out"] = nc.dram_tensor("out", (NT, P, T), F32, kind="ExternalOutput").ap()
    build(nc, **aps)
    r = run_bass_kernel_spmd(nc, [arrays], core_ids=[0])
    return np.asarray(r.results[0]["out"]).reshape(B, C, T)
```

```python
from contextlib import ExitStack

import concourse.bass as bass
import numpy as np
from concourse import mybir

F32 = mybir.dt.float32
F32R = mybir.dt.float32r
I32 = mybir.dt.int32
ALU = mybir.AluOpType
ACT = mybir.ActivationFunctionType

B, C, T = 64, 32, 512
D, HQ, HK = 128, 32, 8
REP = HQ // HK
PAGES, PSIZE, NPP = 64, 32, 16
L = NPP * PSIZE
RANK, LORAS = 16, 32
CONDS = 16
P = 128
BT = P // C
NT = B // BT
HC = T // P
KW = (NPP + 1) * PSIZE
PW = 5 * P
QKB = HQ // 4 + HK // 4
VB = HK // 4
UG = BT * HK
NU = B * HK
SPLIT_AT = 5
SPLIT_LAG = 4
LAG = 3
ROT = 9
WO_HEADS = [0, 5, 5, 5, 5, 5, 5, 2]

SCALE = 1.0 / float(np.sqrt(D))
EPS = 1e-6
NEG = -1e30
TWO_PI = 2.0 * np.pi
C1 = 6.28125
C2 = float(np.float32(1.93500518798828125e-3))
C3 = float(np.float32(TWO_PI - 6.28125 - 1.93500518798828125e-3))
ROUND = 1.5 * 2.0 ** 23
PI_IN = float(np.nextafter(np.float32(np.pi), np.float32(0)))


def ge(eng, sem, val):
    if not isinstance(val, int) or val > 0:
        eng.wait_ge(sem, val)


def build(nc, x, cond_row, id_row, bt_row, idx_pages, seq_tok, seq_all, w0, w3, wb, bias,
          lora_a, lora_b, wqk, wv, wo, qn, kn, kT_cache, v_cache, ident_c, iota_c, row_c, invf_c,
          hmask_c, out):
    ctx = ExitStack()
    with ctx:
        def sb(name, shape, dt=F32):
            return ctx.enter_context(nc.sbuf_tensor(name, shape, dt))

        def rounded(name, region_at, offset, n):
            return nc.alloc_sbuf_tensor_at(name, [P, n], F32R, offset=region_at + 4 * offset)

        def sem(name):
            return ctx.enter_context(nc.semaphore(name))

        qkT_d = nc.dram_tensor("qkT_d", (B, D, QKB, P), F32, kind="Internal").ap()
        v_d = nc.dram_tensor("v_d", (NT * P, HK * D), F32, kind="Internal").ap()
        x2_d = nc.dram_tensor("x2_d", (NT, P, T), F32, kind="Internal").ap()

        atA = -(-nc.sbuf_base // 32) * 32
        regA = sb("regA", [P, HQ * T])
        x2T_hi, x2T_lo = (rounded(f"x2T_{part}", atA, i * HC * NT * P, HC * NT * P)[:, :].rearrange("p (c n) -> p c n", c=HC)
                          for i, part in enumerate(("hi", "lo")))
        wo_sb = regA[:, :].rearrange("p (h n) -> p h n", h=HQ)
        KSZ, VSZ = (NPP + 1) * HK * PSIZE, 5 * HK * D
        KV = KSZ + VSZ
        regK = sb("regK", [P, 2 * KV])
        k_sb = [regK[:, i * KV:i * KV + KSZ].rearrange("p (s h t) -> p s h t", s=NPP + 1, h=HK) for i in range(2)]
        v_sb = [regK[:, i * KV + KSZ:(i + 1) * KV].rearrange("p (k n) -> p k n", k=5) for i in range(2)]
        tabs = regK[:, KV:KV + 4 * NT * D].rearrange("p (k t d) -> p k t d", k=4, t=NT)
        at = [0]

        def inK(n):
            at[0] += n
            assert at[0] <= 2 * KV
            return regK[:, at[0] - n:at[0]]

        x2_sb = [inK(T) for _ in range(4)]
        wb_sb = inK(HC * T).rearrange("p (c n) -> p c n", c=HC)
        x_sb = [inK(T) for _ in range(4)]
        x1_sb = [inK(T) for _ in range(4)]
        x1T_sb = [inK(T) for _ in range(4)]
        bd0 = [inK(P) for _ in range(4)]
        a4 = [inK(BT * HC * RANK).rearrange("p (c n) -> p c n", c=HC) for _ in range(4)]
        b4 = [inK(T) for _ in range(4)]
        hT = [inK(P) for _ in range(4)]
        w0_sb = inK(CONDS * C).rearrange("p (k d) -> p k d", k=CONDS)
        la_sb = inK(LORAS * HC * RANK).rearrange("p (k n) -> p k n", k=LORAS)
        CSZ = 27 * T
        atC = -(-nc.sbuf_base // 32) * 32
        regC = sb("regC", [P, CSZ])
        at[0] = 0

        def inC(n):
            at[0] += n
            assert at[0] <= CSZ
            return regC[:, at[0] - n:at[0]]

        def parts(name, n):
            at[0] += n
            assert at[0] <= CSZ
            return rounded(name, atC, at[0] - n, n)[:, :]

        w_hi = [parts(f"w_hi{i}", HC * T) for i in range(2)]
        w_raw = [regC[:, at[0] + i * HC * T:at[0] + (i + 1) * HC * T] for i in range(2)]
        w_lo = [parts(f"w_lo{i}", HC * T) for i in range(2)]
        t12 = [inC(T) for _ in range(4)]
        t1_sb = [t12[i].rearrange("p (h d) -> p h d", h=4) for i in range(2)]
        t2_sb = [t12[2 + i].rearrange("p (h d) -> p h d", h=4) for i in range(2)]
        trig = [regC[:, 4 * HC * T + i * NT * (D // 2):4 * HC * T + (i + 1) * NT * (D // 2)] for i in range(2)]
        qr_sb = [inC(T) for _ in range(4)]
        st_sb = [inC(T) for _ in range(2)]
        sq_sb = inC(T)
        qn_sb = qr_sb[0].rearrange("p (k d) -> p k d", k=4)[:, 0:2, :]
        hmask = qr_sb[0][0:BT * RANK, 2 * P:3 * P]
        invf, seqi = qr_sb[0][:, 3 * P:3 * P + D // 2], qr_sb[0][:, 3 * P + D // 2:4 * P].bitcast(I32)
        idxi = qr_sb[1][:, 0:B * 4].bitcast(I32)
        at[0] = 0
        oT = inC(HQ * P).rearrange("p (h n) -> p h n", h=HQ)
        p_sb = [inC(PW) for _ in range(4)]
        pT_sb = [inC(PW) for _ in range(2)]
        x2r = inC(T)
        x3_sb = inC(T)
        q_sb = [inC(HK * P) for _ in range(2)]
        k_hi, k_lo, q_hi, q_lo = ([parts(f"{name}{i}", n) for i in range(2)]
                                  for name, n in (("k_hi", KW), ("k_lo", KW), ("q_hi", P), ("q_lo", P)))
        mask = [sb(f"mask{i}", [P, KW]) for i in range(2)]
        ident = sb("ident", [P, P])
        iota = sb("iota", [P, L])
        rowc = sb("rowc", [P, 1])
        seqt = sb("seqt", [P, NT], I32)
        pos = sb("pos", [P, NT])
        seqf = sb("seqf", [P, B])
        HD = D // 2
        ang, turns, red = (regK[:, KV + (i + 4) * NT * HD:KV + (i + 5) * NT * HD] for i in range(3))
        idx_all = sb("idx_all", [P, B * 4], I32)
        idx = [sb(f"idx{i}", [P, 4], I32) for i in range(4)]
        cond = sb("cond", [1, B], I32)
        ids = sb("ids", [1, B], I32)
        btab = sb("btab", [1, B * NPP], I32)
        w3_sb = sb("w3_sb", [P, CONDS, C])
        bd3 = sb("bd3", [P, P])
        ss = sb("ss", [P, 4, 4])
        sd = sb("sd", [P, 4, 4])
        rstd = sb("rstd", [P, 4, 4])
        epsc = sb("epsc", [P, 1])
        nmx = sb("nmx", [P, 4])
        rs = sb("rs", [P, 4])
        rinv = sb("rinv", [P, 4])
        hold = sb("hold", [P, 4])

        S = [ctx.enter_context(nc.psum_tensor(f"S{i}", [P, 1024], F32)) for i in range(2)]
        bank4 = [ctx.enter_context(nc.psum_tensor(f"bank{i}", [P, 512], F32)) for i in range(4, 8)]
        bank = [S[0][:, 0:512], S[0][:, 512:1024], S[1][:, 0:512], S[1][:, 512:1024]] + [b[:, :] for b in bank4]
        pTA, pTB, oP, yP = bank[4:8]
        S0 = 512 - 9 * PSIZE
        scores = [S[i][:, S0:S0 + KW] for i in range(2)]

        s_small, s_rope_in = sem("s_small"), sem("s_rope_in")
        s_wts = sem("s_wts")
        s_xin = [sem(f"s_xin{j}") for j in range(4)]
        s_ones, s_zero = sem("s_ones"), sem("s_zero")
        s_pick = [sem(f"s_pick{j}") for j in range(4)]
        s_pick0 = [sem(f"s_pick0{j}") for j in range(4)]
        s_mm0, s_x1, s_tx1, s_x1T = sem("s_mm0"), sem("s_x1"), sem("s_tx1"), sem("s_x1T")
        s_hmm, s_hT, s_mm1, s_x2 = sem("s_hmm"), sem("s_hT"), sem("s_mm1"), sem("s_x2")
        s_tx2, s_x2T = sem("s_tx2"), sem("s_x2T")
        s_x2st = [sem(f"s_x2st{j}") for j in range(4)]
        s_ang, s_sin, s_tab, s_dve = sem("s_ang"), sem("s_sin"), sem("s_tab"), sem("s_dve")
        s_vz, s_pad, s_idx0 = sem("s_vz"), sem("s_pad"), sem("s_idx0")
        s_w, s_whi, s_wlo = sem("s_w"), sem("s_whi"), sem("s_wlo")
        s_x2lo = sem("s_x2lo")
        s_khi, s_klo = sem("s_khi"), sem("s_klo")
        s_vp, s_vc = sem("s_vp"), sem("s_vc")
        s_vst = [sem(f"s_vst{i}") for i in range(2)]
        s_pj, s_ss, s_sd, s_rstd = sem("s_pj"), sem("s_ss"), sem("s_sd"), sem("s_rstd")
        s_rot, s_qr, s_tq, s_qT = sem("s_rot"), sem("s_qr"), sem("s_tq"), sem("s_qT")
        s_qst = [sem(f"s_qst{i}") for i in range(2)]
        s_wo_in, s_idx = sem("s_wo_in"), sem("s_idx")
        s_k = [sem(f"s_k{i}") for i in range(2)]
        s_v = [sem(f"s_v{i}") for i in range(2)]
        s_vs = [sem(f"s_vs{i}") for i in range(2)]
        s_mask, s_qk, s_mx, s_exp = sem("s_mask"), sem("s_qk"), sem("s_mx"), sem("s_exp")
        s_ri, s_p, s_ta, s_tb = sem("s_ri"), sem("s_p"), sem("s_ta"), sem("s_tb")
        s_evA, s_evB, s_pv, s_oev = sem("s_evA"), sem("s_evB"), sem("s_pv"), sem("s_oev")
        s_wo, s_x3, s_bd3, s_l3 = sem("s_wo"), sem("s_x3"), sem("s_bd3"), sem("s_l3")
        s_out, s_outst, s_x2r = sem("s_out"), sem("s_outst"), sem("s_x2r")
        SMALL = 16 * 8
        WTS = 16 * 4
        KLOAD = 16 * (NPP + 2)
        block = ctx.enter_context(nc.Block())

        @block.sync
        def _(sp):
            SP = [mybir.EngineType.SP]
            for dst, src in ((seqt[:], seq_tok), (invf, invf_c), (rowc[:], row_c), (qn_sb[:, 0, :], qn), (qn_sb[:, 1, :], kn)):
                sp.dma_start(dst, src).then_inc(s_rope_in, 16)
            for dst, src in ((cond[:], cond_row), (ids[:], id_row), (btab[:], bt_row), (ident[:], ident_c), (hmask, hmask_c),
                             (iota[:], iota_c), (seqi, seq_all), (idxi, idx_pages)):
                sp.dma_start(dst, src).then_inc(s_small, 16)
            for dst, src in ((w0_sb, w0), (w3_sb[:], w3), (la_sb, lora_a), (wb_sb, wb)):
                sp.dma_start(dst, src).then_inc(s_wts, 16)
            for j in range(4):
                sp.dma_start(b4[j][BT * RANK:BT * RANK + 1, :], bias).then_inc(s_wts, 16)
            sp.wait_ge(s_small, SMALL)

            def load_tile(i, j):
                sp.dma_start(x_sb[j], x[bass.ds(i * 4 + j, 1)].rearrange("a p n -> p (a n)")).then_inc(s_xin[j], 16)
                _, rows = nc.values_load_multi_w_load_instructions(
                    ids[0:1, bass.ds(i * 16 + 4 * j, BT)], engines=SP, min_val=0, max_val=LORAS - 1)
                for b in range(BT):
                    sp.dma_start(b4[j][b * RANK:(b + 1) * RANK, :],
                                 lora_b[bass.ds(rows[b], 1)].rearrange("a r n -> r (a n)")).then_inc(s_xin[j], 16)

            for j in range(4):
                load_tile(0, j)
            sp.dma_start(w_raw[0], wv[0].rearrange("p c n -> p (c n)")).then_inc(s_w, 16)
            sp.wait_ge(s_w, 16)
            sp.dma_start(w_raw[1], wv[1].rearrange("p c n -> p (c n)")).then_inc(s_w, 16)
            with sp.Fori(1, NT // 4) as i:
                for j in range(4):
                    sp.wait_ge(s_x1, i * 4 - 3 + j)
                    sp.wait_ge(s_mm1, i * 4 - 3 + j)
                    load_tile(i, j)

            for j in range(VB):
                for t in range(NT):
                    sp.wait_ge(s_vc, j * NT + t + 1)
                    sp.dma_start(v_d[t * P:(t + 1) * P, j * T:(j + 1) * T], st_sb[t % 2]).then_inc(s_vst[t % 2], 16)
                sp.wait_ge(s_vp, (j + 1) * NT)
                sp.wait_ge(s_w, 16 * (2 + j))
                sp.dma_start(w_raw[j], wqk[j].rearrange("p c n -> p (c n)")).then_inc(s_w, 16)

            def load_pages(b, par):
                _, pages = nc.values_load_multi_w_load_instructions(
                    btab[0:1, bass.ds(b * NPP, NPP)], engines=SP, min_val=0, max_val=PAGES - 1)
                for n in range(NPP):
                    sp.dma_start(k_sb[par][:, n, :, :].rearrange("p h t -> p (h t)"),
                                 kT_cache[bass.ds(pages[n], 1)].rearrange("a p n -> p (a n)")).then_inc(s_k[par], 16)

            def load_own(b, par):
                sp.dma_start(k_sb[par][:, NPP, :, :].rearrange("p h t -> p (h t)"),
                             qkT_d[bass.ds(b, 1), :, HK:QKB, :].rearrange("a p e n -> p (a e n)")).then_inc(s_k[par], 16)
                sp.dma_start(q_sb[par][:, :],
                             qkT_d[bass.ds(b, 1), :, 0:HK, :].rearrange("a p e n -> p (a e n)")).then_inc(s_k[par], 16)

            def load_own_v(b, par):
                sp.dma_start(v_sb[par][0:C, 4, :], v_d[bass.ds(b * C, C), :]).then_inc(s_vs[par], 16)

            sp.wait_ge(s_x2T, NT)
            for j in range(4):
                sp.wait_ge(s_x2st[j], 16 * (NT // 4))
            load_pages(0, 0)

            def store_qk(e, t):
                sp.wait_ge(s_qT, e * NT + t + 1)
                sp.dma_start(qkT_d[t * BT:(t + 1) * BT, :, bass.ds(e, 1), :].rearrange("b p a n -> p b (a n)"),
                             st_sb[t % 2].rearrange("p (b n) -> p b n", b=BT)).then_inc(s_qst[t % 2], 16)

            with sp.Fori(0, (QKB - 2) // 2) as ee:
                for k in range(2):
                    e = ee * 2 + k
                    for t in range(NT):
                        store_qk(e, t)
                        if t == NT - LAG:
                            sp.dma_start(w_raw[k],
                                         wqk[bass.ds(e + 2, 1)].rearrange("a p c n -> p (a c n)")).then_inc(s_w, 16)
            with sp.Fori(QKB - 2, QKB) as e:
                for t in range(NT):
                    store_qk(e, t)

            for j in range(2):
                sp.wait_ge(s_qst[j], 16 * QKB * NT // 2)
                sp.wait_ge(s_vst[j], 16 * VB * NT // 2)
            load_own(0, 0)
            sp.wait_ge(s_vz, 1)
            load_own_v(0, 0)
            load_pages(1, 1)
            load_own(1, 1)
            sp.wait_ge(s_vz, 2)
            load_own_v(1, 1)
            for h in range(4):
                sp.dma_start(wo_sb[:, h * 8:(h + 1) * 8, :], wo[:, h * 8:(h + 1) * 8, :]).then_inc(s_wo_in, 16)

            def group(g, first, last):
                for k in range(2 if last else 4):
                    b = g * 4 + (k + 2)
                    par = k % 2
                    sp.wait_ge(s_klo, g * UG + HK * (k + 1))
                    load_pages(b, par)
                    load_own(b, par)
                    sp.wait_ge(s_pv, g * UG + HK * (k + 1))
                    load_own_v(b, par)
                    if k == 1 and not first:
                        sp.wait_ge(s_out, g)
                        sp.dma_start(out[bass.ds(g - 1, 1)].rearrange("a p n -> p (a n)"), x3_sb).then_inc(s_outst, 16)
                ge(sp, s_outst, g * 16)
                sp.dma_start(x2r, x2_d[bass.ds(g, 1)].rearrange("a p n -> p (a n)")).then_inc(s_x2r, 16)

            group(0, True, False)
            with sp.Fori(1, NT - 1) as g:
                group(g, False, False)
            group(NT - 1, False, True)
            sp.wait_ge(s_out, NT)
            sp.dma_start(out[NT - 1], x3_sb).then_inc(s_outst, 16)
            sp.wait_ge(s_outst, 16 * NT)

        @block.gpsimd
        def _(pool):
            PL = [mybir.EngineType.Pool]
            pool.wait_ge(s_small, SMALL)
            pool.wait_ge(s_wts, 2 * WTS)

            def pick(i, j):
                ge(pool, s_hmm, i * 4 - 3 + j)
                _, rows = nc.values_load_multi_w_load_instructions(
                    ids[0:1, bass.ds(i * 16 + 4 * j, BT)], engines=PL, min_val=0, max_val=LORAS - 1)
                for b in range(BT):
                    nc.gpsimd.tensor_copy(a4[j][:, :, b * RANK:(b + 1) * RANK],
                                          la_sb[:, bass.ds(rows[b], 1), :].rearrange("p a (c r) -> p (a c) r", c=HC))\
                        .then_inc(s_pick[j], 1)

            for j in range(4):
                pick(0, j)
            with pool.Fori(1, NT // 4) as i:
                for j in range(4):
                    pick(i, j)

            pool.wait_ge(s_x2T, NT)
            for j in range(4):
                pool.wait_ge(s_x2st[j], 16 * (NT // 4))
            nc.gpsimd.memset(v_sb[0][:, 4, :], 0.0).then_inc(s_vz, 1)

            def next_idx(b, k):
                nc.gpsimd.tensor_copy(idx[k][:], idx_all[:, bass.ds(b * 4, 4)]).then_inc(s_idx, 1)

            def gather_v(k, par):
                for m in range(4):
                    nc.gpsimd.indirect_dma_start(
                        out=v_sb[par][:, m, :], out_offset=None, in_=v_cache,
                        in_offset=bass.IndirectOffsetOnAxis(ap=idx[k][:, m:m + 1], axis=0)).then_inc(s_v[par], 16)

            pool.wait_ge(s_idx0, 1)
            next_idx(0, 0)
            next_idx(1, 1)
            next_idx(2, 2)
            pool.wait_ge(s_idx, 2)
            gather_v(0, 0)

            def add_halves(e, t):
                pool.wait_ge(s_rot, e * NT + t + 1)
                ge(pool, s_tq, e * NT + t - 3)
                qv = qr_sb[t % 4].rearrange("p (h d) -> p h d", h=4)
                for lo, hi in ((0, HD), (HD, 0)):
                    nc.gpsimd.tensor_tensor(qv[:, :, lo:lo + HD], t1_sb[t % 2][:, :, lo:lo + HD],
                                            t2_sb[t % 2][:, :, hi:hi + HD], ALU.add).then_inc(s_qr, 1)

            for t in range(NT):
                add_halves(0, t)
            with pool.Fori(1, QKB) as e:
                for t in range(NT):
                    add_halves(e, t)

            pool.wait_ge(s_tq, QKB * NT)
            for i in range(4):
                nc.gpsimd.memset(p_sb[i][:, KW:PW], 0.0).then_inc(s_pad, 1)
            nc.gpsimd.memset(v_sb[1][:, 4, :], 0.0).then_inc(s_vz, 1)
            gather_v(1, 1)

            def group(g, last):
                for k in range(2 if last else 4):
                    b = g * 4 + (k + 2)
                    pool.wait_ge(s_idx, b + 1)
                    pool.wait_ge(s_pv, g * UG + HK * (k + 1))
                    if not (last and k == 1):
                        next_idx(b + 1, (k + 3) % 4)
                    gather_v((k + 2) % 4, k % 2)

            group(0, False)
            with pool.Fori(1, NT - 1) as g:
                group(g, False)
            group(NT - 1, True)

        @block.scalar
        def _(act):
            def pick(dst, table, tile, done):
                _, cs = nc.values_load_multi_w_load_instructions(
                    cond[0:1, bass.ds(tile * BT, BT)], engines=[mybir.EngineType.Activation], min_val=0, max_val=CONDS - 1)
                for b in range(BT):
                    at = slice(b * C, (b + 1) * C)
                    nc.scalar.copy(dst[at, at], table[at, bass.ds(cs[b], 1), :].rearrange("p a d -> p (a d)")).then_inc(done, 1)

            def tile1a(i, last):
                for j in range(4):
                    act.wait_ge(s_tx1, i * 4 + j + 1)
                    nc.scalar.copy(x1T_sb[j], bank[4 + j]).then_inc(s_x1T, 1)
                    if not last:
                        pick(bd0[j], w0_sb, i * 4 + (4 + j), s_pick0[j])
                for j in range(4):
                    act.wait_ge(s_tx2, i * 4 + j + 1)
                    nc.scalar.copy(x2T_hi[:, :, bass.ds((i * 4 + j) * P, P)],
                                   bank[4 + j].rearrange("p (c n) -> p c n", c=HC)).then_inc(s_x2T, 1)
                    act.dma_start(x2_d[bass.ds(i * 4 + j, 1)].rearrange("a p n -> p (a n)"), x2_sb[j]).then_inc(s_x2st[j], 16)

            act.wait_ge(s_small, SMALL)
            act.wait_ge(s_wts, 2 * WTS)
            act.wait_ge(s_zero, 5)
            for j in range(4):
                pick(bd0[j], w0_sb, j, s_pick0[j])
            def split_w(block, k, c):
                if c == 0:
                    act.wait_ge(s_w, 16 * block + 16)
                at = slice(c * T, (c + 1) * T)
                nc.scalar.copy(w_hi[k][:, at], w_raw[k][:, at]).then_inc(s_whi, 1)

            tile1a(0, False)
            for k in range(2):
                for c in range(HC):
                    split_w(k, k, c)
            with act.Fori(1, NT // 4 - 1) as i:
                tile1a(i, False)
            tile1a(NT // 4 - 1, True)

            for j in range(VB):
                for t in range(NT):
                    u = j * NT + t
                    act.wait_ge(s_vp, u + 1)
                    ge(act, s_vst[t % 2], 16 * (u // 2))
                    nc.scalar.copy(st_sb[t % 2], bank[t % 4]).then_inc(s_vc, 1)
                    if j == 1 and 0 <= t - SPLIT_AT < HC:
                        split_w(VB, 0, t - SPLIT_AT)
                if j == 0:
                    for k in range(2):
                        act.wait_ge(s_ang, k + 1)
                        nc.scalar.activation(trig[k], trig[k], ACT.Sin).then_inc(s_sin, 1)

            def squares(e, t):
                act.wait_ge(s_pj, e * NT + t + 1)
                for h in range(4):
                    last = nc.scalar.activation(sq_sb[:, h * D:(h + 1) * D], bank[t % 4][:, h * D:(h + 1) * D], ACT.Square,
                                                accum_out=ss[:, t % 4, h:h + 1])
                last.then_inc(s_ss, 1)
                act.wait_ge(s_ss, e * NT + t + 1)
                nc.scalar.activation(sd[:, t % 4, :], ss[:, t % 4, :], ACT.Sqrt, bias=epsc[:], scale=1.0 / D).then_inc(s_sd, 1)

            def evac(e, t):
                act.wait_ge(s_tq, e * NT + t + 1)
                ge(act, s_qst[t % 2], e * 128 + 16 * (t // 2))
                nc.scalar.copy(st_sb[t % 2].rearrange("p (b h s) -> p h b s", b=BT, h=4),
                               bank[4 + t % 2].rearrange("p (h b s) -> p h b s", h=4, b=BT)).then_inc(s_qT, 1)

            def ahead(e, t):
                return (e, t + LAG) if t + LAG < NT else (e + 1, t + LAG - NT)

            for j in range(2):
                act.wait_ge(s_vst[j], 16 * VB * NT // 2)
            act.wait_ge(s_tab, 1)
            for t in range(LAG):
                squares(0, t)
            def block_qk(e, k):
                for t in range(NT):
                    squares(*ahead(e, t))
                    evac(e, t)
                    if 0 <= t - SPLIT_AT < HC:
                        split_w(e + (VB + 1), 1 - k, t - SPLIT_AT)

            block_qk(0, 0)
            with act.Fori(0, QKB // 2 - 1) as ee:
                block_qk(ee * 2 + 1, 1)
                block_qk(ee * 2 + 2, 0)
            for t in range(NT):
                if t + LAG < NT:
                    squares(QKB - 1, t + LAG)
                evac(QKB - 1, t)

            def split_k(n, u, pair):
                b, h = u // HK % 2, u % HK
                if h == 0:
                    act.wait_ge(s_k[b], pair * KLOAD + KLOAD)
                ge(act, s_qk, n - 1)
                nc.scalar.copy(k_hi[u % 2].rearrange("p (s t) -> p s t", t=PSIZE), k_sb[b][:, :, h, :])
                nc.scalar.copy(q_hi[u % 2], q_sb[b][:, h * P:(h + 1) * P]).then_inc(s_khi, 1)

            def exps(n, u):
                act.wait_ge(s_mx, n + 1)
                nc.scalar.activation(p_sb[u % 4][:, 0:KW], p_sb[u % 4][:, 0:KW], ACT.Exp, bias=nmx[:, u % 4:u % 4 + 1],
                                     scale=-1.0, accum_out=rs[:, u % 4:u % 4 + 1]).then_inc(s_exp, 1)

            def out_head(n, u):
                act.wait_ge(s_pv, n + 1)
                b, h = u // HK % BT, u % HK
                nc.scalar.copy(oT[:, h * REP:(h + 1) * REP, b * C:(b + 1) * C],
                               oP[:, 0:P].rearrange("p (r s) -> p r s", r=REP)).then_inc(s_oev, 1)

            def step(g, u):
                n = g * UG + u
                if not (isinstance(n, int) and n + 4 >= NU):
                    split_k(n + 4, u + 4, g * 2 + (u + 4) // (2 * HK))
                act.wait_ge(s_ta, n + 1)
                ge(act, s_pv, n - 1)
                nc.scalar.copy(pT_sb[u % 2][:, 0:4 * P], pTA).then_inc(s_evA, 1)
                if not (isinstance(n, int) and n + 2 >= NU):
                    exps(n + 2, u + 2)
                if not (isinstance(n, int) and n == 0):
                    out_head(n - 1, (u - 1) % UG)
                if u == ROT + 1:
                    pick(bd3, w3_sb, g, s_bd3)

            for u in range(2):
                split_k(u, u, 0)
            for u in range(2):
                exps(u, u)
                split_k(u + 2, u + 2, 0)
            for u in range(ROT):
                step(0, u)
            with act.Fori(0, NT - 1) as g:
                for u in range(ROT, UG):
                    step(g, u)
                for u in range(ROT):
                    step(g + 1, u)
            for u in range(ROT, UG):
                step(NT - 1, u)
            out_head(NU - 1, UG - 1)

        @block.vector
        def _(dve):
            chain = [0]

            def link(ins):
                chain[0] += 1
                ins.then_inc(s_dve, 1)
                dve.wait_ge(s_dve, chain[0])

            def tile1a(i):
                for j in range(4):
                    dve.wait_ge(s_mm0, i * 4 + j + 1)
                    nc.vector.tensor_tensor(x1_sb[j], bank[j], x_sb[j], ALU.add).then_inc(s_x1, 1)
                for j in range(4):
                    dve.wait_ge(s_hmm, i * 4 + j + 1)
                    nc.vector.tensor_tensor(hT[j][0:BT * RANK, :], bank[4 + j][0:BT * RANK, 0:P], hmask, ALU.mult)\
                        .then_inc(s_hT, 1)
                for j in range(4):
                    dve.wait_ge(s_mm1, i * 4 + j + 1)
                    ge(dve, s_tx2, i * 4 - 3 + j)
                    ge(dve, s_x2st[j], i * 16)
                    nc.vector.tensor_tensor(x2_sb[j], bank[j], x1_sb[j], ALU.add).then_inc(s_x2, 1)

            def x2_low(i):
                for j in range(4):
                    at = bass.ds((i * 4 + j) * P, P)
                    dve.wait_ge(s_x2T, i * 4 + j + 1)
                    nc.vector.tensor_tensor(x2T_lo[:, :, at], bank[4 + j].rearrange("p (c n) -> p c n", c=HC),
                                            x2T_hi[:, :, at].bitcast(F32), ALU.subtract).then_inc(s_x2lo, 1)

            def split_w(block, k, c):
                dve.wait_ge(s_whi, block * HC + (c + 1))
                at = slice(c * T, (c + 1) * T)
                nc.vector.tensor_tensor(w_lo[k][:, at], w_raw[k][:, at], w_hi[k][:, at].bitcast(F32), ALU.subtract)\
                    .then_inc(s_wlo, 1)

            for j in range(4):
                nc.vector.memset(bd0[j], 0.0).then_inc(s_zero, 1)
                nc.vector.memset(hT[j][BT * RANK:BT * RANK + 1, :], 1.0).then_inc(s_ones, 1)
            nc.vector.memset(bd3[:], 0.0).then_inc(s_zero, 1)
            dve.wait_ge(s_small, SMALL)
            tile1a(0)
            x2_low(0)
            for k in range(2):
                for c in range(HC):
                    split_w(k, k, c)
            with dve.Fori(1, NT // 4) as i:
                tile1a(i)
                x2_low(i)

            dve.wait_ge(s_rope_in, 16 * 5)
            link(nc.vector.tensor_copy(pos[:], seqt[:]))
            link(nc.vector.tensor_scalar(pos[:], pos[:], rowc[:], None, ALU.add))
            a3 = ang.rearrange("p (t f) -> p t f", t=NT)
            link(nc.vector.tensor_tensor(a3, pos[:, :].unsqueeze(2).to_broadcast([P, NT, HD]),
                                         invf[:, :].unsqueeze(1).to_broadcast([P, NT, HD]), ALU.mult))
            for k, turn in ((0, 0.0), (1, 0.25)):
                link(nc.vector.tensor_scalar(red, ang, 1.0 / TWO_PI, turn, ALU.mult, ALU.add))
                link(nc.vector.tensor_scalar(turns, red, ROUND, None, ALU.add))
                link(nc.vector.tensor_scalar(turns, turns, ROUND, None, ALU.subtract))
                link(nc.vector.scalar_tensor_tensor(out=red, in0=turns, scalar=-C1, in1=ang, op0=ALU.mult, op1=ALU.add))
                link(nc.vector.scalar_tensor_tensor(out=red, in0=turns, scalar=-C2, in1=red, op0=ALU.mult, op1=ALU.add))
                link(nc.vector.scalar_tensor_tensor(out=red, in0=turns, scalar=-C3, in1=red, op0=ALU.mult, op1=ALU.add))
                link(nc.vector.tensor_scalar(red, red, turn * TWO_PI, PI_IN, ALU.add, ALU.min))
                nc.vector.tensor_scalar(trig[k], red, -PI_IN, None, ALU.max).then_inc(s_ang, 1)
                dve.wait_ge(s_ang, k + 1)
            for c in range(HC):
                split_w(VB, 0, c)
            for i in range(2):
                nc.vector.memset(mask[i][:, L:KW], 0.0)
            nc.vector.tensor_copy(seqf[:], seqi)
            nc.vector.tensor_scalar(idx_all[:], idxi, float(PSIZE), rowc[:], ALU.mult, ALU.add).then_inc(s_idx0, 1)
            dve.wait_ge(s_sin, 2)
            sin3, cos3 = (trig[k].rearrange("p (t f) -> p t f", t=NT) for k in range(2))
            for k in range(2):
                for half, sign in ((0, 1.0), (HD, -1.0)):
                    w = qn_sb[:, k, half:half + HD].unsqueeze(1).to_broadcast([P, NT, HD])
                    nc.vector.tensor_tensor(tabs[:, 2 * k, :, half:half + HD], cos3, w, ALU.mult)
                    last = nc.vector.scalar_tensor_tensor(out=tabs[:, 2 * k + 1, :, half:half + HD], in0=sin3, scalar=sign,
                                                          in1=w, op0=ALU.mult, op1=ALU.mult)
            link(last)
            nc.vector.memset(epsc[:], EPS).then_inc(s_tab, 1)

            def rotate(e, t, k):
                n = e * NT + t
                dve.wait_ge(s_sd, n + 1)
                nc.vector.reciprocal(rstd[:, t % 4, :], sd[:, t % 4, :]).then_inc(s_rstd, 1)
                ge(dve, s_qr, n * 2 - 2)
                dve.wait_ge(s_rstd, n + 1)
                for m, dst in ((0, t1_sb), (1, t2_sb)):
                    for h in range(4):
                        last = nc.vector.scalar_tensor_tensor(
                            out=dst[t % 2][:, h, :], in0=bank[t % 4][:, h * D:(h + 1) * D], scalar=rstd[:, t % 4, h:h + 1],
                            in1=tabs[:, 2 * k + m, t, :], op0=ALU.mult, op1=ALU.mult)
                last.then_inc(s_rot, 1)

            def block_qk(e, buf, table):
                for t in range(NT):
                    rotate(e, t, table)
                    if 0 <= t - SPLIT_AT - SPLIT_LAG < HC and buf is not None:
                        split_w(e + (VB + 1), 1 - buf, t - SPLIT_AT - SPLIT_LAG)

            block_qk(0, 0, 0)
            with dve.Fori(0, HK // 2 - 1) as ee:
                block_qk(ee * 2 + 1, 1, 0)
                block_qk(ee * 2 + 2, 0, 0)
            block_qk(HK - 1, 1, 0)
            block_qk(HK, 0, 1)
            block_qk(HK + 1, None, 1)

            def make_mask(b, par):
                nc.vector.tensor_scalar(mask[par][:, 0:L], iota[:], seqf[:, bass.ds(b, 1)], NEG, ALU.is_ge, ALU.mult)\
                    .then_inc(s_mask, 1)

            def split_k(n, u):
                b, h = u // HK % 2, u % HK
                dve.wait_ge(s_khi, n + 1)
                nc.vector.tensor_tensor(k_lo[u % 2].rearrange("p (s t) -> p s t", t=PSIZE), k_sb[b][:, :, h, :],
                                        k_hi[u % 2].rearrange("p (s t) -> p s t", t=PSIZE).bitcast(F32), ALU.subtract)
                nc.vector.tensor_tensor(q_lo[u % 2], q_sb[b][:, h * P:(h + 1) * P], q_hi[u % 2].bitcast(F32),
                                        ALU.subtract)\
                    .then_inc(s_klo, 1)

            def masked_max(n, u, b):
                if u % HK == 0:
                    dve.wait_ge(s_mask, b + 1)
                dve.wait_ge(s_qk, n + 1)
                nc.vector.memset(hold[:, u % 4:u % 4 + 1], 0.0)
                nc.vector.tensor_tensor_reduce(
                    out=p_sb[u % 4][:, 0:KW], in0=scores[u % 2], in1=mask[u // HK % 2][:], scale=-SCALE, scalar=3e38,
                    op0=ALU.add, op1=ALU.min, accum_out=nmx[:, u % 4:u % 4 + 1]).then_inc(s_mx, 1)

            def normalise(n, u):
                dve.wait_ge(s_exp, n + 1)
                nc.vector.reciprocal(rinv[:, u % 4:u % 4 + 1], rs[:, u % 4:u % 4 + 1]).then_inc(s_ri, 1)
                dve.wait_ge(s_ri, n + 1)
                nc.vector.tensor_scalar(p_sb[u % 4][:, 0:KW], p_sb[u % 4][:, 0:KW], rinv[:, u % 4:u % 4 + 1], None, ALU.mult)\
                    .then_inc(s_p, 1)

            def residual(g):
                dve.wait_ge(s_wo, g + 1)
                dve.wait_ge(s_x2r, g * 16 + 16)
                nc.vector.tensor_tensor(x3_sb, yP, x2r, ALU.add).then_inc(s_x3, 1)

            def finish(g):
                dve.wait_ge(s_l3, g + 1)
                nc.vector.tensor_tensor(x3_sb, yP, x3_sb, ALU.add).then_inc(s_out, 1)

            def step(g, u, before):
                n = g * UG + u
                last = isinstance(n, int)
                if u % HK == 3 and not (last and n + HK >= NU):
                    make_mask(g * BT + (u // HK + 1), (u // HK + 1) % 2)
                if not (last and n + 2 >= NU):
                    masked_max(n + 2, u + 2, g * BT + (u + 2) // HK)
                dve.wait_ge(s_tb, n + 1)
                ge(dve, s_pv, n - 1)
                nc.vector.tensor_copy(pT_sb[u % 2][:, 4 * P:PW], pTB[:, 0:P]).then_inc(s_evB, 1)
                if not (last and n + 1 >= NU):
                    normalise(n + 1, u + 1)
                if not (last and n + 4 >= NU):
                    split_k(n + 4, u + 4)
                if before is not None and u == ROT - 2:
                    residual(before)
                if before is not None and u == ROT - 1:
                    finish(before)

            make_mask(0, 0)
            for u in range(2):
                split_k(u, u)
            for u in range(2):
                masked_max(u, u, 0)
                split_k(u + 2, u + 2)
            normalise(0, 0)
            for u in range(ROT):
                step(0, u, None)
            with dve.Fori(0, NT - 1) as g:
                for u in range(ROT, UG):
                    step(g, u, None)
                for u in range(ROT):
                    step(g + 1, u, g)
            for u in range(ROT, UG):
                step(NT - 1, u, None)
            residual(NT - 1)
            finish(NT - 1)

        @block.tensor
        def _(pe):
            def transposes(dst, src):
                for c in range(4):
                    last = nc.tensor.transpose(dst[:, c * P:(c + 1) * P], src[:, c * P:(c + 1) * P], ident[:])
                return last

            def tile1a(i):
                for j in range(4):
                    pe.wait_ge(s_pick0[j], i * 4 + 4)
                    pe.wait_ge(s_xin[j], i * 80 + 80)
                    ge(pe, s_x2, i * 4 - 3 + j)
                    nc.tensor.matmul(bank[j], bd0[j], x_sb[j], start=True, stop=True).then_inc(s_mm0, 1)
                for j in range(4):
                    pe.wait_ge(s_x1, i * 4 + j + 1)
                    ge(pe, s_x2lo, i * 4 - 3 + j)
                    transposes(bank[4 + j], x1_sb[j]).then_inc(s_tx1, 1)
                for j in range(4):
                    pe.wait_ge(s_x1T, i * 4 + j + 1)
                    pe.wait_ge(s_pick[j], i * 4 + 4)
                    for c in range(HC):
                        last = nc.tensor.matmul(bank[4 + j][0:BT * RANK, 0:P], a4[j][:, c, :],
                                                x1T_sb[j][:, c * P:(c + 1) * P], start=(c == 0), stop=(c == HC - 1))
                    last.then_inc(s_hmm, 1)
                    for c in range(HC):
                        nc.tensor.matmul(bank[j], x1T_sb[j][:, c * P:(c + 1) * P], wb_sb[:, c, :], start=(c == 0), stop=False)
                for j in range(4):
                    pe.wait_ge(s_hT, i * 4 + j + 1)
                    nc.tensor.matmul(bank[j], hT[j][0:BT * RANK + 1, :], b4[j][0:BT * RANK + 1, :], start=False, stop=True)\
                        .then_inc(s_mm1, 1)
                for j in range(4):
                    pe.wait_ge(s_x2, i * 4 + j + 1)
                    transposes(bank[4 + j], x2_sb[j]).then_inc(s_tx2, 1)

            pe.wait_ge(s_small, SMALL)
            pe.wait_ge(s_wts, 2 * WTS)
            pe.wait_ge(s_ones, 4)
            tile1a(0)
            with pe.Fori(1, NT // 4) as i:
                tile1a(i)

            def project(t, k):
                for c in range(HC):
                    rows, cols = slice(t * P, (t + 1) * P), slice(c * T, (c + 1) * T)
                    for m, (a, w) in enumerate(((x2T_hi, w_hi), (x2T_hi, w_lo), (x2T_lo, w_hi))):
                        last = nc.tensor.matmul(bank[t % 4], a[:, c, rows], w[k][:, cols],
                                                start=(c == 0 and m == 0), stop=(c == HC - 1 and m == 2))
                return last

            for j in range(VB):
                pe.wait_ge(s_wlo, (j + 1) * HC)
                for t in range(NT):
                    if j == 0:
                        pe.wait_ge(s_x2lo, t + 1)
                    ge(pe, s_vc, j * NT + t - 3)
                    project(t, j).then_inc(s_vp, 1)

            def project_qk(e, t, k):
                if t == 0:
                    pe.wait_ge(s_wlo, e * HC + (VB + 1) * HC)
                ge(pe, s_rot, e * NT + t - 3)
                project(t, k).then_inc(s_pj, 1)

            def turn_qk(e, t):
                pe.wait_ge(s_qr, e * (2 * NT) + 2 * t + 2)
                ge(pe, s_qT, e * NT + t - 1)
                transposes(bank[4 + t % 2], qr_sb[t % 4]).then_inc(s_tq, 1)

            def block_qk(e, k, last):
                for t in range(NT):
                    if t + LAG < NT:
                        project_qk(e, t + LAG, k)
                    elif not last:
                        project_qk(e + 1, t + LAG - NT, 1 - k)
                    turn_qk(e, t)

            pe.wait_ge(s_vc, VB * NT)
            for t in range(LAG):
                project_qk(0, t, 0)
            block_qk(0, 0, False)
            with pe.Fori(0, QKB // 2 - 1) as ee:
                block_qk(ee * 2 + 1, 1, False)
                block_qk(ee * 2 + 2, 0, False)
            block_qk(QKB - 1, 1, True)

            def score(n, u):
                pe.wait_ge(s_klo, n + 1)
                ge(pe, s_mx, n - 1)
                halves = (slice(0, 9 * PSIZE), slice(9 * PSIZE, KW))
                for m, (q, k) in enumerate(((q_hi, k_hi), (q_hi, k_lo), (q_lo, k_hi))):
                    for at in halves:
                        last = nc.tensor.matmul(scores[u % 2][:, at], q[u % 2], k[u % 2][:, at],
                                                start=(m == 0), stop=(m == 2))
                last.then_inc(s_qk, 1)

            def turn_p(n, u):
                pe.wait_ge(s_p, n + 1)
                ge(pe, s_evA, n)
                transposes(pTA, p_sb[u % 4]).then_inc(s_ta, 1)
                ge(pe, s_evB, n)
                nc.tensor.transpose(pTB[:, 0:P], p_sb[u % 4][:, 4 * P:PW], ident[:]).then_inc(s_tb, 1)

            def values(n, u, pair):
                b, h = u // HK % 2, u % HK
                if h == 0:
                    pe.wait_ge(s_v[b], pair * 64 + 64)
                    pe.wait_ge(s_vs[b], pair * 16 + 16)
                pe.wait_ge(s_evA, n + 1)
                pe.wait_ge(s_evB, n + 1)
                ge(pe, s_oev, n)
                for m in range(5):
                    last = nc.tensor.matmul(oP[:, 0:P], v_sb[b][:, m, h * D:(h + 1) * D], pT_sb[u % 2][:, m * P:(m + 1) * P],
                                            start=(m == 0), stop=(m == 4))
                last.then_inc(s_pv, 1)

            def out_proj(g, h0, h1):
                if h0 == 0:
                    pe.wait_ge(s_oev, g * UG + UG)
                    pe.wait_ge(s_wo_in, 64)
                for h in range(h0, h1):
                    last = nc.tensor.matmul(yP, oT[:, h, :], wo_sb[:, h, :], start=(h == 0), stop=(h == HQ - 1))
                if h1 == HQ:
                    last.then_inc(s_wo, 1)

            def mix3(g):
                pe.wait_ge(s_x3, g + 1)
                pe.wait_ge(s_bd3, g * BT + BT)
                nc.tensor.matmul(yP, bd3[:], x3_sb, start=True, stop=True).then_inc(s_l3, 1)

            def step(g, u, before):
                n = g * UG + u
                fixed = isinstance(n, int)
                if not (fixed and n + 2 >= NU):
                    score(n + 2, u + 2)
                turn_p(n, u)
                if before is not None and u < len(WO_HEADS):
                    h0 = sum(WO_HEADS[:u])
                    if WO_HEADS[u]:
                        out_proj(before, h0, h0 + WO_HEADS[u])
                if before is not None and u == ROT - 1:
                    mix3(before)
                if not (fixed and n == 0):
                    m = (u - 1) % UG
                    values(n - 1, m, g * 2 + m // (2 * HK) if u else g * 2 - 1)

            score(0, 0)
            score(1, 1)
            pe.wait_ge(s_pad, 4)
            for u in range(ROT):
                step(0, u, None)
            with pe.Fori(0, NT - 1) as g:
                for u in range(ROT, UG):
                    step(g, u, None)
                for u in range(ROT):
                    step(g + 1, u, g)
            for u in range(ROT, UG):
                step(NT - 1, u, None)
            values(NU - 1, UG - 1, 2 * NT - 1)
            out_proj(NT - 1, 0, HQ)
            mix3(NT - 1)


def kernel(x, itok_B_0_15, itok_B_6_15, itok_Bx16_0_63, itok_B_207_1644, L0_cond_weights, L1_cond_base_weight,
           L1_cond_base_bias, L1_cond_lora_A_w, L1_cond_lora_B_w, L2_cond_Wq, L2_cond_Wk, L2_cond_Wv, L2_cond_Wo,
           L2_cond_q_norm_w, L2_cond_k_norm_w, L2_cond_k_cache, L2_cond_v_cache, L3_cond_weights):
    import concourse.bacc as bacc
    from concourse.bass_utils import run_bass_kernel_spmd

    def blocks(w, n):
        return np.asarray(w).reshape(n, T, HC, P).transpose(0, 3, 2, 1)

    bt = np.asarray(itok_Bx16_0_63)
    seq = np.asarray(itok_B_207_1644)
    of_row = np.arange(P) // C
    lora_a = np.asarray(L1_cond_lora_A_w).reshape(LORAS, RANK, HC, P).transpose(3, 0, 2, 1).reshape(P, LORAS, HC * RANK)
    arrays = {
        "x": np.asarray(x).reshape(NT, P, T),
        "cond_row": np.asarray(itok_B_0_15).reshape(1, B),
        "id_row": np.asarray(itok_B_6_15).reshape(1, B),
        "bt_row": bt.reshape(1, B * NPP),
        "idx_pages": np.repeat(bt.reshape(B, 4, 4).transpose(2, 0, 1).reshape(4, B * 4), PSIZE, axis=0),
        "seq_tok": seq.reshape(NT, BT)[:, of_row].T,
        "seq_all": np.repeat(seq.reshape(1, B), P, axis=0),
        "w0": np.tile(np.asarray(L0_cond_weights).transpose(1, 0, 2), (BT, 1, 1)),
        "w3": np.tile(np.asarray(L3_cond_weights).transpose(1, 0, 2), (BT, 1, 1)),
        "wb": np.asarray(L1_cond_base_weight).reshape(T, HC, P).transpose(2, 1, 0),
        "bias": np.asarray(L1_cond_base_bias).reshape(1, T),
        "lora_a": lora_a,
        "lora_b": np.asarray(L1_cond_lora_B_w).transpose(0, 2, 1),
        "wqk": np.concatenate([blocks(L2_cond_Wq, HK), blocks(L2_cond_Wk, HK // 4)]),
        "wv": blocks(L2_cond_Wv, VB),
        "wo": np.asarray(L2_cond_Wo).reshape(T, HQ, D).transpose(2, 1, 0),
        "qn": np.repeat(np.asarray(L2_cond_q_norm_w).reshape(1, D), P, axis=0),
        "kn": np.repeat(np.asarray(L2_cond_k_norm_w).reshape(1, D), P, axis=0),
        "kT_cache": np.asarray(L2_cond_k_cache).transpose(0, 3, 2, 1).reshape(PAGES, D, HK * PSIZE),
        "v_cache": np.asarray(L2_cond_v_cache).reshape(PAGES * PSIZE, HK * D),
        "ident_c": np.eye(P, dtype=np.float32),
        "iota_c": np.tile(np.arange(L, dtype=np.float32), (P, 1)),
        "row_c": (np.arange(P) % C).astype(np.float32).reshape(P, 1),
        "invf_c": np.tile((1.0 / 10000.0 ** (np.arange(0, D, 2) / D)).astype(np.float32), (P, 1)),
        "hmask_c": np.repeat(np.repeat(np.eye(BT, dtype=np.float32), RANK, axis=0), C, axis=1),
    }
    arrays = {k: np.ascontiguousarray(v) for k, v in arrays.items()}
    nc = bacc.Bacc("TRN2", target_bir_lowering=False, num_devices=1)
    aps = {k: nc.dram_tensor(k, v.shape, mybir.dt.from_np(v.dtype), kind="ExternalInput").ap() for k, v in arrays.items()}
    aps["out"] = nc.dram_tensor("out", (NT, P, T), F32, kind="ExternalOutput").ap()
    build(nc, **aps)
    r = run_bass_kernel_spmd(nc, [arrays], core_ids=[0])
    return np.asarray(r.results[0]["out"]).reshape(B, C, T)
```

```python
from contextlib import ExitStack

import concourse.bass as bass
import numpy as np
from concourse import mybir

F32 = mybir.dt.float32
F32R = mybir.dt.float32r
I32 = mybir.dt.int32
ALU = mybir.AluOpType
ACT = mybir.ActivationFunctionType

B, C, T = 64, 32, 512
D, HQ, HK = 128, 32, 8
REP = HQ // HK
PAGES, PSIZE, NPP = 64, 32, 16
L = NPP * PSIZE
RANK, LORAS = 16, 32
CONDS = 16
P = 128
BT = P // C
NT = B // BT
HC = T // P
KW = (NPP + 1) * PSIZE
QKB = HQ // 4 + HK // 4
VB = HK // 4
UG = BT * HK
NU = B * HK
SPLIT_AT = 5
SPLIT_LAG = 4
FIRST_AT = {8: 0, 13: 1}
LAG = 3
ROT = 24
H2 = HQ // 2
WO_AT = {UG - 2: 0, UG - 1: 2, 0: 4, 1: 6, 2: 8, 3: 11, 4: 14, 5: H2}
LOW = 11
WO_SPLIT = 8

SCALE = 1.0 / float(np.sqrt(D))
EPS = 1e-6
NEG = -1e30
TWO_PI = 2.0 * np.pi
C1 = 6.28125
C2 = float(np.float32(1.93500518798828125e-3))
C3 = float(np.float32(TWO_PI - 6.28125 - 1.93500518798828125e-3))
ROUND = 1.5 * 2.0 ** 23
PI_IN = float(np.nextafter(np.float32(np.pi), np.float32(0)))


def ge(eng, sem, val):
    if not isinstance(val, int) or val > 0:
        eng.wait_ge(sem, val)


def build(nc, x, cond_row, id_row, bt_row, idx_pages, seq_tok, seq_all, w0, w3, wb, bias,
          lora_a, lora_b, wqk, wv, wo, qn, kn, kT_cache, v_cache, ident_c, iota_c, row_c, invf_c,
          hmask_c, out):
    ctx = ExitStack()
    with ctx:
        def sb(name, shape, dt=F32):
            return ctx.enter_context(nc.sbuf_tensor(name, shape, dt))

        def rounded(name, region_at, offset, n):
            return nc.alloc_sbuf_tensor_at(name, [P, n], F32R, offset=region_at + 4 * offset)

        def sem(name):
            return ctx.enter_context(nc.semaphore(name))

        qkT_d = nc.dram_tensor("qkT_d", (B, D, QKB, P), F32, kind="Internal").ap()
        v_d = nc.dram_tensor("v_d", (REP, NT * P, VB, D), F32, kind="Internal").ap()
        oT_d = nc.dram_tensor("oT_d", (NT, D, BT, T), F32, kind="Internal").ap()
        x2_d = nc.dram_tensor("x2_d", (NT, P, T), F32, kind="Internal").ap()

        atA = -(-nc.sbuf_base // 32) * 32
        regA = sb("regA", [P, HQ * T])
        x2T_hi, x2T_lo = (rounded(f"x2T_{part}", atA, i * HC * NT * P, HC * NT * P)[:, :].rearrange("p (c n) -> p c n", c=HC)
                          for i, part in enumerate(("hi", "lo")))
        WSZ = H2 * T
        wo_hi, wo_lo = (rounded(f"wo_{part}", atA, i * WSZ, WSZ)[:, :] for i, part in enumerate(("hi", "lo")))
        wo_raw = regA[:, WSZ:2 * WSZ]
        KSZ, VSZ, OSZ = (NPP + 1) * HK * PSIZE, 4 * HK * D, VB * D
        KV = KSZ + VSZ + OSZ
        atK = -(-nc.sbuf_base // 32) * 32
        regK = sb("regK", [P, 2 * KV])
        k_sb = [regK[:, i * KV:i * KV + KSZ].rearrange("p (s h t) -> p s h t", s=NPP + 1, h=HK) for i in range(2)]
        v_sb = [regK[:, i * KV + KSZ:i * KV + KSZ + VSZ].rearrange("p (k n) -> p k n", k=4) for i in range(2)]
        vo_sb = [regK[:, i * KV + KSZ + VSZ:(i + 1) * KV] for i in range(2)]
        wo3_raw = regK[:, 0:WSZ]
        wo3_lo = rounded("wo3_lo", atK, 0, WSZ)[:, :]
        o3_raw = [regK[:, KV + i * H2 * P:KV + (i + 1) * H2 * P] for i in range(2)]
        o3_parts = [rounded(f"o3_{part}", atK, KV + (2 + i) * H2 * P, H2 * P)[:, :] for i, part in enumerate(("hi", "lo"))]
        tabs = regK[:, KV:KV + 4 * NT * D].rearrange("p (k t d) -> p k t d", k=4, t=NT)
        at = [0]

        def inK(n):
            at[0] += n
            assert at[0] <= 2 * KV
            return regK[:, at[0] - n:at[0]]

        x2_sb = [inK(T) for _ in range(4)]
        wb_lo = rounded("wb_lo", atK, at[0], HC * T)[:, :]
        wb_sb = inK(HC * T)
        x_sb = [inK(T) for _ in range(4)]
        x1_sb = [inK(T) for _ in range(4)]
        x1T_sb = [inK(T) for _ in range(4)]
        bd0 = [inK(P) for _ in range(4)]
        a4 = [inK(BT * HC * RANK).rearrange("p (c n) -> p c n", c=HC) for _ in range(4)]
        b4 = [inK(T) for _ in range(4)]
        hT = [inK(P) for _ in range(4)]
        w0_sb = inK(CONDS * C).rearrange("p (k d) -> p k d", k=CONDS)
        la_sb = inK(LORAS * HC * RANK).rearrange("p (k n) -> p k n", k=LORAS)
        CSZ = 27 * T + KW + 2 * P
        atC = -(-nc.sbuf_base // 32) * 32
        regC = sb("regC", [P, CSZ])
        at[0] = 0

        def inC(n):
            at[0] += n
            assert at[0] <= CSZ
            return regC[:, at[0] - n:at[0]]

        def parts(name, n):
            at[0] += n
            assert at[0] <= CSZ
            return rounded(name, atC, at[0] - n, n)[:, :]

        w_hi = [parts(f"w_hi{i}", HC * T) for i in range(2)]
        w_raw = [regC[:, at[0] + i * HC * T:at[0] + (i + 1) * HC * T] for i in range(2)]
        w_lo = [parts(f"w_lo{i}", HC * T) for i in range(2)]
        t12 = [inC(T) for _ in range(4)]
        t1_sb = [t12[i].rearrange("p (h d) -> p h d", h=4) for i in range(2)]
        t2_sb = [t12[2 + i].rearrange("p (h d) -> p h d", h=4) for i in range(2)]
        trig = [regC[:, 4 * HC * T + i * NT * (D // 2):4 * HC * T + (i + 1) * NT * (D // 2)] for i in range(2)]
        wb_hi = rounded("wb_hi", atC, 4 * HC * T, HC * T)[:, :]
        qr_sb = [inC(T) for _ in range(4)]
        x1T_hi, x1T_lo = ([rounded(f"x1T_{part}{i}", atC, at[0] - 2 * T + (2 * k + i) * T, T)[:, :] for i in range(2)]
                          for k, part in enumerate(("hi", "lo")))
        st_sb = [inC(T) for _ in range(2)]
        sq_sb = inC(T)
        qn_sb = qr_sb[0].rearrange("p (k d) -> p k d", k=4)[:, 0:2, :]
        hmask = qr_sb[0][0:BT * RANK, 2 * P:3 * P]
        invf, seqi = qr_sb[0][:, 3 * P:3 * P + D // 2], qr_sb[0][:, 3 * P + D // 2:4 * P].bitcast(I32)
        idxi = qr_sb[1][:, 0:B * 4].bitcast(I32)
        at[0] = 0
        q_sb = [inC(HK * P) for _ in range(2)]
        oT_hi = parts("oT_hi", H2 * P)
        q_hi, q_lo = [parts("q_hi0", P)], [parts("q_lo0", P)]
        k_hi, k_lo = zip(*([parts(f"{name}{i}", KW) for name in ("k_hi", "k_lo")] for i in range(2)))
        o_st = inC(T)
        x2r = inC(T)
        po_sb = [inC(P) for _ in range(2)]
        p_next = [inC(KW) for _ in range(3)]
        pT_sb = [inC(L) for _ in range(2)]
        pTo_sb = inC(4 * P)
        oT_lo = parts("oT_lo", H2 * P)
        at[0] = 27 * T
        p_sb = [inC(KW)] + p_next
        q_hi.append(parts("q_hi1", P))
        q_lo.append(parts("q_lo1", P))
        o3_hi, o3_lo = ((y, x) for x, y in zip((oT_hi, oT_lo), o3_parts))
        xy = [o_st, x2r]
        ones = sb("ones", [P, P])
        mask = [sb(f"mask{i}", [P, KW]) for i in range(2)]
        ident = sb("ident", [P, P])
        iota = sb("iota", [P, L])
        rowc = sb("rowc", [P, 1])
        seqt = sb("seqt", [P, NT], I32)
        pos = sb("pos", [P, NT])
        seqf = sb("seqf", [P, B])
        HD = D // 2
        ang, turns, red = (regK[:, KV + (i + 4) * NT * HD:KV + (i + 5) * NT * HD] for i in range(3))
        idx_all = sb("idx_all", [P, (B + 1) * 4], I32)
        idx = [sb(f"idx{i}", [P, 4], I32) for i in range(4)]
        cond = sb("cond", [1, B], I32)
        ids = sb("ids", [1, B], I32)
        btab = sb("btab", [1, B * NPP], I32)
        w3_sb = sb("w3_sb", [P, CONDS, C])
        bd3 = [pT_sb[i][:, 0:P] for i in range(2)]
        ss = sb("ss", [P, 4, 4])
        sd = sb("sd", [P, 4, 4])
        rstd = sb("rstd", [P, 4, 4])
        epsc = sb("epsc", [P, 1])
        nmx = sb("nmx", [P, 4])
        rs = sb("rs", [P, 4])
        rinv = sb("rinv", [P, 4])
        warm = sb("warm", [P, 2])
        hold = sb("hold", [P, 4])

        S = [ctx.enter_context(nc.psum_tensor(f"S{i}", [P, 1024], F32)) for i in range(2)]
        bank4 = [ctx.enter_context(nc.psum_tensor(f"bank{i}", [P, 512], F32)) for i in range(4, 8)]
        bank = [S[0][:, 0:512], S[0][:, 512:1024], S[1][:, 0:512], S[1][:, 512:1024]] + [b[:, :] for b in bank4]
        pT, oP, yP = bank[4:6], bank[6], bank[7]
        S0 = 512 - 9 * PSIZE
        scores = [S[i][:, S0:S0 + KW] for i in range(2)]

        s_ids, s_const, s_late = sem("s_ids"), sem("s_const"), sem("s_late")
        s_warm = sem("s_warm")
        s_w0, s_la, s_wb, s_bias = sem("s_w0"), sem("s_la"), sem("s_wb"), sem("s_bias")
        s_wbhi, s_wblo = sem("s_wbhi"), sem("s_wblo")
        s_x1hi, s_x1lo = sem("s_x1hi"), sem("s_x1lo")
        s_bin = [sem(f"s_bin{j}") for j in range(4)]
        s_xin = [sem(f"s_xin{j}") for j in range(4)]
        s_ones, s_zero, s_zero3 = sem("s_ones"), sem("s_zero"), sem("s_zero3")
        s_pick = [sem(f"s_pick{j}") for j in range(4)]
        s_pick0 = [sem(f"s_pick0{j}") for j in range(4)]
        s_mm0, s_x1, s_tx1, s_x1T = sem("s_mm0"), sem("s_x1"), sem("s_tx1"), sem("s_x1T")
        s_hmm, s_hT, s_mm1, s_x2 = sem("s_hmm"), sem("s_hT"), sem("s_mm1"), sem("s_x2")
        s_tx2, s_x2T = sem("s_tx2"), sem("s_x2T")
        s_x2st = [sem(f"s_x2st{j}") for j in range(4)]
        s_ang, s_sin, s_tab, s_dve = sem("s_ang"), sem("s_sin"), sem("s_tab"), sem("s_dve")
        s_idx0 = sem("s_idx0")
        s_w, s_whi, s_wlo = sem("s_w"), sem("s_whi"), sem("s_wlo")
        s_x2lo = sem("s_x2lo")
        s_khi, s_klo = sem("s_khi"), sem("s_klo")
        s_vp, s_vc = sem("s_vp"), sem("s_vc")
        s_vst = [sem(f"s_vst{i}") for i in range(2)]
        s_pj, s_ss, s_sd, s_rstd = sem("s_pj"), sem("s_ss"), sem("s_sd"), sem("s_rstd")
        s_rot, s_qr, s_tq, s_qT = sem("s_rot"), sem("s_qr"), sem("s_tq"), sem("s_qT")
        s_qst = [sem(f"s_qst{i}") for i in range(2)]
        s_wo_in, s_wohi, s_wolo = sem("s_wo_in"), sem("s_wohi"), sem("s_wolo")
        s_idx = sem("s_idx")
        s_k = [sem(f"s_k{i}") for i in range(2)]
        s_v = [sem(f"s_v{i}") for i in range(2)]
        s_vs = [sem(f"s_vs{i}") for i in range(2)]
        s_qhi, s_qp = sem("s_qhi"), sem("s_qp")
        s_mask, s_qk, s_mx, s_exp, s_ri, s_p = (sem(f"s_{x}") for x in ("mask", "qk", "mx", "exp", "ri", "p"))
        s_ta, s_tb, s_evA, s_evB = sem("s_ta"), sem("s_tb"), sem("s_evA"), sem("s_evB")
        s_pv, s_po = sem("s_pv"), sem("s_po")
        s_ohi, s_oev, s_ost, s_ostst = sem("s_ohi"), sem("s_oev"), sem("s_ost"), sem("s_ostst")
        s_wo, s_x2r, s_x2y, s_x2yst = sem("s_wo"), sem("s_x2r"), sem("s_x2y"), sem("s_x2yst")
        s_o3 = [sem(f"s_o3{i}") for i in range(2)]
        s_xy = [sem(f"s_xy{i}") for i in range(2)]
        s_o3hi, s_o3lo, s_wo3, s_x3 = sem("s_o3hi"), sem("s_o3lo"), sem("s_wo3"), sem("s_x3")
        s_bd3 = [sem(f"s_bd3{i}") for i in range(2)]
        s_l3, s_out, s_outst = sem("s_l3"), sem("s_out"), sem("s_outst")
        LATE = 16 * 10
        KLOAD = 16 * (NPP + 2)
        block = ctx.enter_context(nc.Block())

        def tile(i, j):
            return i + j // 4, j % 4, i * 4 + j

        def k_low(engine, b, h, u, slots):
            lo, hi = (k[u % 2].rearrange("p (s t) -> p s t", t=PSIZE)[:, slots, :] for k in (k_lo, k_hi))
            return engine.tensor_tensor(lo, k_sb[b][:, slots, h, :], hi.bitcast(F32), ALU.subtract)

        @block.sync
        def _(sp):
            SP = [mybir.EngineType.SP]
            for dst, src in ((cond[:], cond_row), (ids[:], id_row)):
                sp.dma_start(dst, src).then_inc(s_ids, 16)
            sp.dma_start(w0_sb, w0).then_inc(s_w0, 16)

            def load_x(i, j):
                i, j, t = tile(i, j)
                sp.dma_start(x_sb[j], x[bass.ds(t, 1)].rearrange("a p n -> p (a n)")).then_inc(s_xin[j], 16)

            def load_b(i, j):
                i, j, t = tile(i, j)
                _, rows = nc.values_load_multi_w_load_instructions(
                    ids[0:1, bass.ds(t * BT, BT)], engines=SP, min_val=0, max_val=LORAS - 1)
                for b in range(BT):
                    sp.dma_start(b4[j][b * RANK:(b + 1) * RANK, :],
                                 lora_b[bass.ds(rows[b], 1)].rearrange("a r n -> r (a n)")).then_inc(s_bin[j], 16)

            for j in range(2):
                load_x(0, j)
            sp.dma_start(wb_sb, wb.rearrange("p c n -> p (c n)")).then_inc(s_wb, 16)
            sp.dma_start(la_sb, lora_a).then_inc(s_la, 16)
            for j in range(4):
                sp.dma_start(b4[j][BT * RANK:BT * RANK + 1, :], bias).then_inc(s_bias, 16)
            for j in range(2, 4):
                load_x(0, j)
            sp.wait_ge(s_ids, 32)
            for j in range(4):
                load_b(0, j)
            for j in range(4):
                sp.wait_ge(s_x1, j + 1)
                load_x(1, j)
            sp.dma_start(w_raw[0], wv[0].rearrange("p c n -> p (c n)")).then_inc(s_w, 16)
            for j in range(4):
                sp.wait_ge(s_mm1, j + 1)
                load_b(1, j)
            sp.wait_ge(s_w, 16)
            sp.dma_start(w_raw[1], wv[1].rearrange("p c n -> p (c n)")).then_inc(s_w, 16)
            with sp.Fori(2, NT // 4) as i:
                for j in range(4):
                    sp.wait_ge(s_x1, i * 4 - 3 + j)
                    load_x(i, j)
                    sp.wait_ge(s_mm1, i * 4 - 3 + j)
                    load_b(i, j)
            for dst, src in ((seqt[:], seq_tok), (invf, invf_c), (rowc[:], row_c), (qn_sb[:, 0, :], qn), (qn_sb[:, 1, :], kn),
                             (btab[:], bt_row), (iota[:], iota_c), (seqi, seq_all), (idxi, idx_pages), (w3_sb[:], w3)):
                sp.dma_start(dst, src).then_inc(s_late, 16)
            sp.wait_ge(s_late, LATE)

            for j in range(VB):
                for t in range(NT):
                    sp.wait_ge(s_vc, j * NT + t + 1)
                    sp.dma_start(v_d[:, t * P:(t + 1) * P, j, :].rearrange("r p d -> p r d"),
                                 st_sb[t % 2].rearrange("p (r d) -> p r d", r=REP)).then_inc(s_vst[t % 2], 16)
                sp.wait_ge(s_vp, (j + 1) * NT)
                sp.wait_ge(s_w, 16 * (2 + j))
                sp.dma_start(w_raw[j], wqk[j].rearrange("p c n -> p (c n)")).then_inc(s_w, 16)

            def load_pages(b, par, first=0, count=NPP):
                _, pages = nc.values_load_multi_w_load_instructions(
                    btab[0:1, bass.ds(b * NPP + first, count)], engines=SP, min_val=0, max_val=PAGES - 1)
                for n in range(count):
                    sp.dma_start(k_sb[par][:, first + n, :, :].rearrange("p h t -> p (h t)"),
                                 kT_cache[bass.ds(pages[n], 1)].rearrange("a p n -> p (a n)")).then_inc(s_k[par], 16)

            def load_own(b, par):
                sp.dma_start(k_sb[par][:, NPP, :, :].rearrange("p h t -> p (h t)"),
                             qkT_d[bass.ds(b, 1), :, HK:QKB, :].rearrange("a p e n -> p (a e n)")).then_inc(s_k[par], 16)
                sp.dma_start(q_sb[par][:, :],
                             qkT_d[bass.ds(b, 1), :, 0:HK, :].rearrange("a p e n -> p (a e n)")).then_inc(s_k[par], 16)

            def load_own_v(b, par):
                for r in range(REP):
                    sp.dma_start(vo_sb[par][r * C:(r + 1) * C, :],
                                 v_d[r, bass.ds(b * C, C), :, :].rearrange("p j d -> p (j d)")).then_inc(s_vs[par], 16)

            sp.wait_ge(s_x2T, NT)
            for j in range(4):
                sp.wait_ge(s_x2st[j], 16 * (NT // 4))
            load_pages(0, 0)

            def store_qk(e, t):
                sp.wait_ge(s_qT, e * NT + t + 1)
                sp.dma_start(qkT_d[t * BT:(t + 1) * BT, :, bass.ds(e, 1), :].rearrange("b p a n -> p b (a n)"),
                             st_sb[t % 2].rearrange("p (b n) -> p b n", b=BT)).then_inc(s_qst[t % 2], 16)

            with sp.Fori(0, (QKB - 2) // 2) as ee:
                for k in range(2):
                    e = ee * 2 + k
                    for t in range(NT):
                        store_qk(e, t)
                        if t == NT - LAG:
                            sp.dma_start(w_raw[k],
                                         wqk[bass.ds(e + 2, 1)].rearrange("a p c n -> p (a c n)")).then_inc(s_w, 16)
            for t in range(NT):
                store_qk(QKB - 2, t)
            for t in range(NT):
                store_qk(QKB - 1, t)
                if t == 2:
                    for j in range(2):
                        sp.wait_ge(s_vst[j], 16 * VB * NT // 2)
                    sp.wait_ge(s_qst[0], 16 * ((QKB - 1) * NT // 2 + 1))
                    load_own(0, 0)
                    load_own_v(0, 0)
                if 4 <= t < 12:
                    load_pages(1, 1, (t - 4) * 2, 2)
            load_own(1, 1)
            load_own_v(1, 1)
            for j in range(2):
                sp.wait_ge(s_qst[j], 16 * QKB * NT // 2)
            sp.dma_start(wo_raw, wo[0]).then_inc(s_wo_in, 16)

            def group(g, first, last):
                for k in range(BT):
                    b = g * BT + (k + 2)
                    if not (last and k >= 2):
                        sp.wait_ge(s_qp, g * UG + HK * (k + 1))
                        load_own(b, k % 2)
                        sp.wait_ge(s_klo, g * UG + HK * (k + 1))
                        load_pages(b, k % 2)
                        sp.wait_ge(s_po, g * (2 * BT) + 2 * (k + 1))
                        load_own_v(b, k % 2)
                    sp.wait_ge(s_ost, g * BT + (k + 1))
                    sp.dma_start(oT_d[bass.ds(g, 1), :, k, :].rearrange("a p n -> p (a n)"), o_st).then_inc(s_ostst, 16)
                    if last and k == 2:
                        sp.wait_ge(s_klo, NU - HK)
                        sp.wait_ge(s_qp, NU - HK)
                        sp.wait_ge(s_po, NU // 4 - 2)
                        sp.dma_start(wo3_raw, wo[1]).then_inc(s_wo_in, 16)
                    if k == 0 and not first:
                        sp.wait_ge(s_x2y, g)
                        sp.dma_start(x2_d[bass.ds(g - 1, 1)].rearrange("a p n -> p (a n)"), x2r).then_inc(s_x2yst, 16)
                    if k == 1:
                        ge(sp, s_x2yst, g * 16)
                        sp.dma_start(x2r, x2_d[bass.ds(g, 1)].rearrange("a p n -> p (a n)")).then_inc(s_x2r, 16)

            group(0, True, False)
            with sp.Fori(1, NT - 1) as g:
                group(g, False, False)
            group(NT - 1, False, True)

            sp.wait_ge(s_klo, NU)
            sp.wait_ge(s_qp, NU)
            sp.wait_ge(s_po, NU // 4)
            sp.wait_ge(s_ostst, 16 * 3 * BT)

            def load_o(g, i):
                sp.dma_start(o3_raw[i], oT_d[bass.ds(g, 1)].rearrange("a p b n -> p (a b n)")).then_inc(s_o3[i], 16)

            def load_xy(g, i):
                sp.dma_start(xy[i], x2_d[bass.ds(g, 1)].rearrange("a p n -> p (a n)")).then_inc(s_xy[i], 16)

            def store_out(g, i):
                sp.wait_ge(s_out, g + 1)
                sp.dma_start(out[bass.ds(g, 1)].rearrange("a p n -> p (a n)"), xy[i]).then_inc(s_outst, 16)

            for i in range(2):
                load_o(i, i)
            sp.wait_ge(s_x2y, NT)
            sp.dma_start(x2_d[NT - 1], x2r).then_inc(s_x2yst, 16)
            sp.wait_ge(s_x2yst, 16 * NT)
            for i in range(2):
                load_xy(i, i)
            sp.wait_ge(s_ostst, 16 * B)
            sp.wait_ge(s_o3lo, 1)
            load_o(2, 0)

            def turn_over(g, i, ahead):
                if ahead:
                    sp.wait_ge(s_o3lo, g + 2)
                    load_o(g + 3, 1 - i)
                store_out(g, i)
                sp.wait_ge(s_outst, g * 16 + 16)
                load_xy(g + 2, i)

            with sp.Fori(0, NT // 2 - 2) as gg:
                for i in range(2):
                    turn_over(gg * 2 + i, i, True)
            turn_over(NT - 4, 0, True)
            turn_over(NT - 3, 1, False)
            for i in range(2):
                store_out(NT - 2 + i, i)
            sp.wait_ge(s_outst, 16 * NT)

        @block.gpsimd
        def _(pool):
            PL = [mybir.EngineType.Pool]
            pool.wait_ge(s_ids, 32)
            pool.wait_ge(s_la, 16)

            def pick(i, j):
                ge(pool, s_hmm, i * 4 - 3 + j)
                _, rows = nc.values_load_multi_w_load_instructions(
                    ids[0:1, bass.ds(i * 16 + 4 * j, BT)], engines=PL, min_val=0, max_val=LORAS - 1)
                for b in range(BT):
                    nc.gpsimd.tensor_copy(a4[j][:, :, b * RANK:(b + 1) * RANK],
                                          la_sb[:, bass.ds(rows[b], 1), :].rearrange("p a (c r) -> p (a c) r", c=HC))\
                        .then_inc(s_pick[j], 1)

            for j in range(4):
                pick(0, j)
            with pool.Fori(1, NT // 4) as i:
                for j in range(4):
                    pick(i, j)

            pool.wait_ge(s_x2T, NT)
            for j in range(4):
                pool.wait_ge(s_x2st[j], 16 * (NT // 4))
            def next_idx(b, k):
                nc.gpsimd.tensor_copy(idx[k][:], idx_all[:, bass.ds(b * 4, 4)]).then_inc(s_idx, 1)

            def gather_v(k, par, m):
                nc.gpsimd.indirect_dma_start(
                    out=v_sb[par][:, m, :], out_offset=None, in_=v_cache,
                    in_offset=bass.IndirectOffsetOnAxis(ap=idx[k][:, m:m + 1], axis=0)).then_inc(s_v[par], 16)

            nc.gpsimd.memset(ones[:], 1.0).then_inc(s_ones, 1)
            pool.wait_ge(s_ones, 5)
            pool.wait_ge(s_idx0, 1)
            next_idx(0, 0)
            next_idx(1, 1)
            next_idx(2, 2)
            pool.wait_ge(s_idx, 2)
            for m in range(4):
                gather_v(0, 0, m)

            def add_halves(e, t):
                pool.wait_ge(s_rot, e * NT + t + 1)
                ge(pool, s_tq, e * NT + t - 3)
                qv = qr_sb[t % 4].rearrange("p (h d) -> p h d", h=4)
                for lo, hi in ((0, HD), (HD, 0)):
                    nc.gpsimd.tensor_tensor(qv[:, :, lo:lo + HD], t1_sb[t % 2][:, :, lo:lo + HD],
                                            t2_sb[t % 2][:, :, hi:hi + HD], ALU.add).then_inc(s_qr, 1)

            for t in range(NT):
                add_halves(0, t)
            with pool.Fori(1, QKB - 1) as e:
                for t in range(NT):
                    add_halves(e, t)
            def split_q(n, u, pair):
                b, h = u // HK % 2, u % HK
                if h == 0:
                    pool.wait_ge(s_k[b], pair * KLOAD + KLOAD)
                ge(pool, s_qk, n - 1)
                q = q_sb[b][:, h * P:(h + 1) * P]
                nc.gpsimd.tensor_tensor(q_hi[u % 2], q, ones[:], ALU.mult).then_inc(s_qhi, 1)
                pool.wait_ge(s_qhi, n + 1)
                nc.gpsimd.tensor_tensor(q_lo[u % 2], q, q_hi[u % 2].bitcast(F32), ALU.subtract)
                pool.wait_ge(s_khi, n + 1)
                k_low(nc.gpsimd, b, h, u, slice(LOW, NPP + 1)).then_inc(s_qp, 1)

            def step(g, u):
                n = g * UG + u
                fixed = isinstance(n, int)
                if not (fixed and n + 4 >= NU):
                    split_q(n + 4, u + 4, g * 2 + (u + 4) // (2 * HK))
                k, m = (u - 10) // HK, (u - 10) % HK
                if m < 4 and not (fixed and not 2 <= g * BT + k + 2 < B):
                    if m == 0:
                        b = g * BT + (k + 2)
                        pool.wait_ge(s_idx, b + 1)
                        pool.wait_ge(s_po, g * (2 * BT) + 2 * (k + 1))
                        next_idx(b + 1, (k + 3) % 4)
                    gather_v((k + 2) % 4, k % 2, m)

            for t in range(NT):
                add_halves(QKB - 1, t)
                if t in (NT - 4, NT - 2):
                    u = (t - (NT - 4)) // 2
                    split_q(u, u, 0)
            for u in range(2, 4):
                split_q(u, u, 0)
            pool.wait_ge(s_tq, QKB * NT)
            nc.gpsimd.memset(pTo_sb, 0.0).then_inc(s_ones, 1)
            for u in range(ROT):
                step(0, u)
                if 2 <= u < 6:
                    gather_v(1, 1, u - 2)
            with pool.Fori(0, NT - 1) as g:
                for u in range(ROT, UG):
                    step(g, u)
                for u in range(ROT):
                    step(g + 1, u)
            for u in range(ROT, UG):
                step(NT - 1, u)
            pool.wait_ge(s_po, NU // 4)
            for i in range(2):
                nc.gpsimd.memset(bd3[i], 0.0).then_inc(s_zero3, 1)

        @block.scalar
        def _(act):
            def pick(dst, table, tile, done):
                _, cs = nc.values_load_multi_w_load_instructions(
                    cond[0:1, bass.ds(tile * BT, BT)], engines=[mybir.EngineType.Activation], min_val=0, max_val=CONDS - 1)
                for b in range(BT):
                    at = slice(b * C, (b + 1) * C)
                    nc.scalar.copy(dst[at, at], table[at, bass.ds(cs[b], 1), :].rearrange("p a d -> p (a d)")).then_inc(done, 1)

            def x1_turned(i, j):
                i, j, t = tile(i, j)
                act.wait_ge(s_tx1, t + 1)
                nc.scalar.copy(x1T_sb[j], bank[4]).then_inc(s_x1T, 1)
                act.wait_ge(s_x1T, t + 1)
                nc.scalar.copy(x1T_hi[j % 2], x1T_sb[j]).then_inc(s_x1hi, 1)

            def pick0(i, j):
                i, j, t = tile(i, j)
                pick(bd0[j], w0_sb, t, s_pick0[j])

            def x2_turned(i, j):
                i, j, t = tile(i, j)
                act.wait_ge(s_tx2, t + 1)
                nc.scalar.copy(x2T_hi[:, :, bass.ds(t * P, P)],
                               bank[6 + j % 2].rearrange("p (c n) -> p c n", c=HC)).then_inc(s_x2T, 1)
                act.dma_start(x2_d[bass.ds(t, 1)].rearrange("a p n -> p (a n)"), x2_sb[j]).then_inc(s_x2st[j], 16)

            def split_w(block, k, c):
                if c == 0:
                    act.wait_ge(s_w, 16 * block + 16)
                at = slice(c * T, (c + 1) * T)
                nc.scalar.copy(w_hi[k][:, at], w_raw[k][:, at]).then_inc(s_whi, 1)

            def round1a(i, first, last):
                for j in range(4):
                    if not (last and j == 3):
                        x1_turned(i, j + 1)
                    if not last:
                        pick0(i, j + 4)
                    if not (first and j == 0):
                        x2_turned(i, j - 1)
                    if last:
                        for c in range(2):
                            split_w(j // 2, j // 2, j % 2 * 2 + c)

            for dst, src in ((ident[:], ident_c), (hmask, hmask_c)):
                act.dma_start(dst, src).then_inc(s_const, 16)
            act.wait_ge(s_warm, 1)
            nc.scalar.copy(warm[:, 1:2], warm[:, 0:1])
            act.wait_ge(s_ids, 32)
            act.wait_ge(s_w0, 16)
            act.wait_ge(s_zero, 4)
            for j in range(4):
                pick0(0, j)
            x1_turned(0, 0)
            act.wait_ge(s_wb, 16)
            for c in range(HC):
                nc.scalar.copy(wb_hi[:, c * T:(c + 1) * T], wb_sb[:, c * T:(c + 1) * T]).then_inc(s_wbhi, 1)
            round1a(0, True, False)
            with act.Fori(1, NT // 4 - 1) as i:
                round1a(i, False, False)
            round1a(NT // 4 - 1, False, True)
            x2_turned(NT // 4 - 1, 3)

            for j in range(VB):
                for t in range(NT):
                    u = j * NT + t
                    act.wait_ge(s_vp, u + 1)
                    ge(act, s_vst[t % 2], 16 * (u // 2))
                    nc.scalar.copy(st_sb[t % 2], bank[t % 4]).then_inc(s_vc, 1)
                    if j == 1 and 0 <= t - SPLIT_AT < HC:
                        split_w(VB, 0, t - SPLIT_AT)
                if j == 0:
                    for k in range(2):
                        act.wait_ge(s_ang, k + 1)
                        nc.scalar.activation(trig[k], trig[k], ACT.Sin).then_inc(s_sin, 1)

            def squares(e, t):
                act.wait_ge(s_pj, e * NT + t + 1)
                for h in range(4):
                    last = nc.scalar.activation(sq_sb[:, h * D:(h + 1) * D], bank[t % 4][:, h * D:(h + 1) * D], ACT.Square,
                                                accum_out=ss[:, t % 4, h:h + 1])
                last.then_inc(s_ss, 1)
                act.wait_ge(s_ss, e * NT + t + 1)
                nc.scalar.activation(sd[:, t % 4, :], ss[:, t % 4, :], ACT.Sqrt, bias=epsc[:], scale=1.0 / D).then_inc(s_sd, 1)

            def evac(e, t):
                act.wait_ge(s_tq, e * NT + t + 1)
                ge(act, s_qst[t % 2], e * 128 + 16 * (t // 2))
                nc.scalar.copy(st_sb[t % 2].rearrange("p (b h s) -> p h b s", b=BT, h=4),
                               bank[4 + t % 2].rearrange("p (h b s) -> p h b s", h=4, b=BT)).then_inc(s_qT, 1)

            def ahead(e, t):
                return (e, t + LAG) if t + LAG < NT else (e + 1, t + LAG - NT)

            for j in range(2):
                act.wait_ge(s_vst[j], 16 * VB * NT // 2)
            act.wait_ge(s_tab, 1)
            for t in range(LAG):
                squares(0, t)
            def block_qk(e, k):
                for t in range(NT):
                    squares(*ahead(e, t))
                    evac(e, t)
                    if 0 <= t - SPLIT_AT < HC:
                        split_w(e + (VB + 1), 1 - k, t - SPLIT_AT)

            block_qk(0, 0)
            with act.Fori(0, QKB // 2 - 1) as ee:
                block_qk(ee * 2 + 1, 1)
                block_qk(ee * 2 + 2, 0)
            def split_k(n, u, pair):
                b, h = u // HK % 2, u % HK
                if h == 0:
                    act.wait_ge(s_k[b], pair * KLOAD + KLOAD)
                ge(act, s_qk, n - 1)
                nc.scalar.copy(k_hi[u % 2].rearrange("p (s t) -> p s t", t=PSIZE), k_sb[b][:, :, h, :]).then_inc(s_khi, 1)

            def exps(n, u):
                act.wait_ge(s_mx, n + 1)
                p = p_sb[u % 4]
                nc.scalar.activation(p, p, ACT.Exp, bias=nmx[:, u % 4:u % 4 + 1],
                                     scale=-1.0, accum_out=rs[:, u % 4:u % 4 + 1]).then_inc(s_exp, 1)

            def out_heads(g, u):
                q = (u - 4) // 4
                act.wait_ge(s_po, g * HK + (q + 1))
                if q % 2 == 0:
                    if q == 0:
                        ge(act, s_wo, g)
                    b = q // 2
                    nc.scalar.copy(oT_hi.rearrange("p (r n) -> p r n", n=P)[:, :, b * C:(b + 1) * C],
                                   oP.rearrange("p (r s) -> p r s", s=C)).then_inc(s_ohi, 1)
                else:
                    ge(act, s_ostst, g * (16 * BT) + 16 * (q // 2))
                    nc.scalar.copy(o_st, oP).then_inc(s_ost, 1)

            def split_wo(half, h, raw):
                if h == 0:
                    act.wait_ge(s_wo_in, 16 * half + 16)
                at = slice(h * T, (h + 1) * T)
                nc.scalar.copy(wo_hi[:, at], raw[:, at]).then_inc(s_wohi, 1)

            def step(g, u):
                n = g * UG + u
                fixed = isinstance(n, int)
                if not (fixed and n + 4 >= NU):
                    split_k(n + 4, u + 4, g * 2 + (u + 4) // (2 * HK))
                if u % 4 == 0:
                    if not (fixed and n + 2 >= NU):
                        exps(n + 2, u + 2)
                    if not (fixed and n == 0):
                        out_heads(g, u)
                act.wait_ge(s_ta, n + 1)
                ge(act, s_pv, n - 1)
                nc.scalar.copy(pT_sb[u % 2], pT[u % 2]).then_inc(s_evA, 1)
                if u % 4 == 3:
                    act.wait_ge(s_tb, g * HK + (u // 4 + 1))
                    ge(act, s_po, g * HK + u // 4)
                    for r in range(4):
                        rows = slice(r * C, (r + 1) * C)
                        last = nc.scalar.copy(pTo_sb[rows, r * P:(r + 1) * P], pT[0][rows, 0:P])
                    last.then_inc(s_evB, 1)
                if u % 4 and not (fixed and n + 2 >= NU):
                    exps(n + 2, u + 2)

            for t in range(NT):
                if t + LAG < NT:
                    squares(QKB - 1, t + LAG)
                if t in FIRST_AT:
                    split_k(FIRST_AT[t], FIRST_AT[t], 0)
                if t == NT - LAG:
                    nc.scalar.activation(warm[:, 1:2], warm[:, 0:1], ACT.Exp)
                if t == NT - 1:
                    exps(0, 0)
                    split_k(2, 2, 0)
                evac(QKB - 1, t)
            exps(1, 1)
            split_k(3, 3, 0)
            for u in range(ROT):
                if u == 3:
                    act.wait_ge(s_ones, 6)
                step(0, u)
                if 0 <= u - WO_SPLIT < H2:
                    split_wo(0, u - WO_SPLIT, wo_raw)
            with act.Fori(0, NT - 1) as g:
                for u in range(ROT, UG):
                    step(g, u)
                for u in range(ROT):
                    step(g + 1, u)
            for u in range(ROT, UG):
                step(NT - 1, u)
            out_heads(NT - 1, UG)

            def high(g, i):
                act.wait_ge(s_o3[i], (g - i) * 8 + 16)
                ge(act, s_wo3, g - 1)
                nc.scalar.copy(o3_hi[i].rearrange("p (r b s) -> p b r s", b=BT, s=C),
                               o3_raw[i].rearrange("p (b r s) -> p b r s", b=BT, s=C)).then_inc(s_o3hi, 1)
                ge(act, s_l3, g - 1)
                pick(bd3[i], w3_sb, g, s_bd3[i])

            act.wait_ge(s_late, LATE)
            act.wait_ge(s_zero3, 2)
            high(0, 0)
            act.wait_ge(s_wo, NT)
            for h in range(H2):
                split_wo(1, h, wo3_raw)
            high(1, 1)
            with act.Fori(1, NT // 2) as gg:
                for i in range(2):
                    high(gg * 2 + i, i)

        @block.vector
        def _(dve):
            chain = [0]

            def link(ins):
                chain[0] += 1
                ins.then_inc(s_dve, 1)
                dve.wait_ge(s_dve, chain[0])

            def add0(i, j):
                i, j, t = tile(i, j)
                dve.wait_ge(s_mm0, t + 1)
                nc.vector.tensor_tensor(x1_sb[j], bank[j % 2], x_sb[j], ALU.add).then_inc(s_x1, 1)

            def x1_low(i, j):
                i, j, t = tile(i, j)
                dve.wait_ge(s_x1hi, t + 1)
                nc.vector.tensor_tensor(x1T_lo[j % 2], x1T_sb[j], x1T_hi[j % 2].bitcast(F32), ALU.subtract).then_inc(s_x1lo, 1)

            def own_rank(i, j):
                i, j, t = tile(i, j)
                dve.wait_ge(s_hmm, t + 1)
                nc.vector.tensor_tensor(hT[j][0:BT * RANK, :], bank[5][0:BT * RANK, 0:P], hmask, ALU.mult).then_inc(s_hT, 1)

            def add1(i, j):
                i, j, t = tile(i, j)
                dve.wait_ge(s_mm1, t + 1)
                ge(dve, s_x2st[j], i * 16)
                nc.vector.tensor_tensor(x2_sb[j], bank[2 + j % 2], x1_sb[j], ALU.add).then_inc(s_x2, 1)

            def x2_low(i, j):
                i, j, t = tile(i, j)
                at = bass.ds(t * P, P)
                dve.wait_ge(s_x2T, t + 1)
                nc.vector.tensor_tensor(x2T_lo[:, :, at], bank[6 + j % 2].rearrange("p (c n) -> p c n", c=HC),
                                        x2T_hi[:, :, at].bitcast(F32), ALU.subtract).then_inc(s_x2lo, 1)

            def split_w(block, k, c):
                dve.wait_ge(s_whi, block * HC + (c + 1))
                at = slice(c * T, (c + 1) * T)
                nc.vector.tensor_tensor(w_lo[k][:, at], w_raw[k][:, at], w_hi[k][:, at].bitcast(F32), ALU.subtract)\
                    .then_inc(s_wlo, 1)

            nc.vector.memset(warm[:], 0.0).then_inc(s_warm, 1)
            for j in range(4):
                nc.vector.memset(bd0[j], 0.0).then_inc(s_zero, 1)
                nc.vector.memset(hT[j][BT * RANK:BT * RANK + 1, :], 1.0).then_inc(s_ones, 1)
            def round1a(i, first, last):
                for j in range(4):
                    if not (last and j >= 2):
                        add0(i, j + 2)
                    own_rank(i, j)
                    if not (last and j == 3):
                        x1_low(i, j + 1)
                    if not (first and j == 0):
                        x2_low(i, j - 1)
                    if last:
                        for c in range(2):
                            split_w(j // 2, j // 2, j % 2 * 2 + c)
                    add1(i, j)

            for j in range(2):
                add0(0, j)
            x1_low(0, 0)
            for c in range(HC):
                dve.wait_ge(s_wbhi, c + 1)
                at = slice(c * T, (c + 1) * T)
                nc.vector.tensor_tensor(wb_lo[:, at], wb_sb[:, at], wb_hi[:, at].bitcast(F32), ALU.subtract).then_inc(s_wblo, 1)
            dve.wait_ge(s_const, 32)
            round1a(0, True, False)
            with dve.Fori(1, NT // 4 - 1) as i:
                round1a(i, False, False)
            round1a(NT // 4 - 1, False, True)
            x2_low(NT // 4 - 1, 3)

            dve.wait_ge(s_late, LATE)
            link(nc.vector.tensor_copy(pos[:], seqt[:]))
            link(nc.vector.tensor_scalar(pos[:], pos[:], rowc[:], None, ALU.add))
            a3 = ang.rearrange("p (t f) -> p t f", t=NT)
            link(nc.vector.tensor_tensor(a3, pos[:, :].unsqueeze(2).to_broadcast([P, NT, HD]),
                                         invf[:, :].unsqueeze(1).to_broadcast([P, NT, HD]), ALU.mult))
            for k, turn in ((0, 0.0), (1, 0.25)):
                link(nc.vector.tensor_scalar(red, ang, 1.0 / TWO_PI, turn, ALU.mult, ALU.add))
                link(nc.vector.tensor_scalar(turns, red, ROUND, None, ALU.add))
                link(nc.vector.tensor_scalar(turns, turns, ROUND, None, ALU.subtract))
                link(nc.vector.scalar_tensor_tensor(out=red, in0=turns, scalar=-C1, in1=ang, op0=ALU.mult, op1=ALU.add))
                link(nc.vector.scalar_tensor_tensor(out=red, in0=turns, scalar=-C2, in1=red, op0=ALU.mult, op1=ALU.add))
                link(nc.vector.scalar_tensor_tensor(out=red, in0=turns, scalar=-C3, in1=red, op0=ALU.mult, op1=ALU.add))
                link(nc.vector.tensor_scalar(red, red, turn * TWO_PI, PI_IN, ALU.add, ALU.min))
                nc.vector.tensor_scalar(trig[k], red, -PI_IN, None, ALU.max).then_inc(s_ang, 1)
                dve.wait_ge(s_ang, k + 1)
            for c in range(HC):
                split_w(VB, 0, c)
            for i in range(2):
                nc.vector.memset(mask[i][:, L:KW], 0.0)
            nc.vector.tensor_copy(seqf[:], seqi)
            nc.vector.memset(idx_all[:, B * 4:], 0.0)
            nc.vector.tensor_scalar(idx_all[:, 0:B * 4], idxi, float(PSIZE), rowc[:], ALU.mult, ALU.add).then_inc(s_idx0, 1)
            dve.wait_ge(s_sin, 2)
            sin3, cos3 = (trig[k].rearrange("p (t f) -> p t f", t=NT) for k in range(2))
            for k in range(2):
                for half, sign in ((0, 1.0), (HD, -1.0)):
                    w = qn_sb[:, k, half:half + HD].unsqueeze(1).to_broadcast([P, NT, HD])
                    nc.vector.tensor_tensor(tabs[:, 2 * k, :, half:half + HD], cos3, w, ALU.mult)
                    last = nc.vector.scalar_tensor_tensor(out=tabs[:, 2 * k + 1, :, half:half + HD], in0=sin3, scalar=sign,
                                                          in1=w, op0=ALU.mult, op1=ALU.mult)
            link(last)
            nc.vector.memset(epsc[:], EPS).then_inc(s_tab, 1)

            def rotate(e, t, k):
                n = e * NT + t
                dve.wait_ge(s_sd, n + 1)
                nc.vector.reciprocal(rstd[:, t % 4, :], sd[:, t % 4, :]).then_inc(s_rstd, 1)
                ge(dve, s_qr, n * 2 - 2)
                dve.wait_ge(s_rstd, n + 1)
                for m, dst in ((0, t1_sb), (1, t2_sb)):
                    for h in range(4):
                        last = nc.vector.scalar_tensor_tensor(
                            out=dst[t % 2][:, h, :], in0=bank[t % 4][:, h * D:(h + 1) * D], scalar=rstd[:, t % 4, h:h + 1],
                            in1=tabs[:, 2 * k + m, t, :], op0=ALU.mult, op1=ALU.mult)
                last.then_inc(s_rot, 1)

            def block_qk(e, buf, table):
                for t in range(NT):
                    rotate(e, t, table)
                    if buf is None and t == NT - 4:
                        make_mask(0, 0)
                        split_k(0, 0)
                    if 0 <= t - SPLIT_AT - SPLIT_LAG < HC and buf is not None:
                        split_w(e + (VB + 1), 1 - buf, t - SPLIT_AT - SPLIT_LAG)

            def make_mask(b, par):
                nc.vector.tensor_scalar(mask[par][:, 0:L], iota[:], seqf[:, bass.ds(b, 1)], NEG, ALU.is_ge, ALU.mult)\
                    .then_inc(s_mask, 1)

            def split_k(n, u):
                b, h = u // HK % 2, u % HK
                dve.wait_ge(s_khi, n + 1)
                k_low(nc.vector, b, h, u, slice(0, LOW)).then_inc(s_klo, 1)

            def masked_max(n, u, b):
                if u % HK == 0:
                    dve.wait_ge(s_mask, b + 1)
                dve.wait_ge(s_qk, n + 1)
                nc.vector.memset(hold[:, u % 4:u % 4 + 1], 0.0)
                nc.vector.tensor_tensor_reduce(
                    out=p_sb[u % 4], in0=scores[u % 2], in1=mask[u // HK % 2][:], scale=-SCALE, scalar=3e38,
                    op0=ALU.add, op1=ALU.min, accum_out=nmx[:, u % 4:u % 4 + 1]).then_inc(s_mx, 1)

            def inverse(n, u):
                dve.wait_ge(s_exp, n + 1)
                nc.vector.reciprocal(rinv[:, u % 4:u % 4 + 1], rs[:, u % 4:u % 4 + 1]).then_inc(s_ri, 1)

            def normalise(n, u):
                dve.wait_ge(s_ri, n + 1)
                p, j = p_sb[u % 4], u % 4
                nc.vector.tensor_scalar(po_sb[u // 4 % 2][:, j * C:(j + 1) * C], p[:, L:KW], rinv[:, j:j + 1], None, ALU.mult)
                nc.vector.tensor_scalar(p[:, 0:L], p[:, 0:L], rinv[:, j:j + 1], None, ALU.mult).then_inc(s_p, 1)

            def out_low(g, b):
                dve.wait_ge(s_ohi, g * BT + (b + 1))
                at = slice(b * C, (b + 1) * C)
                nc.vector.tensor_tensor(oT_lo.rearrange("p (r n) -> p r n", n=P)[:, :, at], oP.rearrange("p (r s) -> p r s", s=C),
                                        oT_hi.rearrange("p (r n) -> p r n", n=P)[:, :, at].bitcast(F32), ALU.subtract)\
                    .then_inc(s_oev, 1)

            def residual(g):
                dve.wait_ge(s_wo, g + 1)
                dve.wait_ge(s_x2r, g * 16 + 16)
                nc.vector.tensor_tensor(x2r, yP, x2r, ALU.add).then_inc(s_x2y, 1)

            def split_wo(half, h, lo, raw):
                dve.wait_ge(s_wohi, half * H2 + h + 1)
                at = slice(h * T, (h + 1) * T)
                nc.vector.tensor_tensor(lo[:, at], raw[:, at], wo_hi[:, at].bitcast(F32), ALU.subtract).then_inc(s_wolo, 1)

            def step(g, u, before):
                n = g * UG + u
                fixed = isinstance(n, int)
                if u % HK == 3 and not (fixed and n + HK >= NU):
                    make_mask(g * BT + (u // HK + 1), (u // HK + 1) % 2)
                if not (fixed and n + 1 >= NU):
                    inverse(n + 1, u + 1)
                if not (fixed and n + 2 >= NU):
                    masked_max(n + 2, u + 2, g * BT + (u + 2) // HK)
                if not (fixed and n + 1 >= NU):
                    normalise(n + 1, u + 1)
                if not (fixed and n + 4 >= NU):
                    split_k(n + 4, u + 4)
                if u % HK == 4:
                    out_low(g, u // HK)
                if before is not None and u == 6:
                    residual(before)

            block_qk(0, 0, 0)
            with dve.Fori(0, HK // 2 - 1) as ee:
                block_qk(ee * 2 + 1, 1, 0)
                block_qk(ee * 2 + 2, 0, 0)
            block_qk(HK - 1, 1, 0)
            block_qk(HK, 0, 1)
            block_qk(HK + 1, None, 1)

            split_k(1, 1)
            for u in range(2):
                masked_max(u, u, 0)
                split_k(u + 2, u + 2)
            inverse(0, 0)
            normalise(0, 0)
            for u in range(ROT):
                if u == 4:
                    for j in range(2):
                        dve.wait_ge(s_qst[j], 16 * QKB * NT // 2)
                step(0, u, None)
                if 0 <= u - WO_SPLIT < H2:
                    split_wo(0, u - WO_SPLIT, wo_lo, wo_raw)
            with dve.Fori(0, NT - 1) as g:
                for u in range(ROT, UG):
                    step(g, u, None)
                for u in range(ROT):
                    step(g + 1, u, g)
            for u in range(ROT, UG):
                step(NT - 1, u, None)

            def low(g, i):
                dve.wait_ge(s_o3hi, g + 1)
                nc.vector.tensor_tensor(o3_lo[i].rearrange("p (r b s) -> p b r s", b=BT, s=C),
                                        o3_raw[i].rearrange("p (b r s) -> p b r s", b=BT, s=C),
                                        o3_hi[i].rearrange("p (r b s) -> p b r s", b=BT, s=C).bitcast(F32), ALU.subtract)\
                    .then_inc(s_o3lo, 1)

            def residual3(g, i):
                dve.wait_ge(s_wo3, g + 1)
                dve.wait_ge(s_xy[i], (g - i) * 8 + 16)
                nc.vector.tensor_tensor(xy[i], bank[i], xy[i], ALU.add).then_inc(s_x3, 1)

            def finish(g, i):
                dve.wait_ge(s_l3, g + 1)
                nc.vector.tensor_tensor(xy[i], bank[2 + i], xy[i], ALU.add).then_inc(s_out, 1)

            low(0, 0)
            residual(NT - 1)
            for h in range(H2):
                split_wo(1, h, wo3_lo, wo3_raw)
            low(1, 1)
            residual3(0, 0)
            with dve.Fori(0, NT // 2 - 1) as gg:
                for i in range(2):
                    low(gg * 2 + (i + 2), i)
                    residual3(gg * 2 + (i + 1), 1 - i)
                    finish(gg * 2 + i, i)
            residual3(NT - 1, 1)
            for i in range(2):
                finish(NT - 2 + i, i)

        @block.tensor
        def _(pe):
            def transposes(dst, src):
                for c in range(4):
                    last = nc.tensor.transpose(dst[:, c * P:(c + 1) * P], src[:, c * P:(c + 1) * P], ident[:])
                return last

            def mix0(i, j):
                i, j, t = tile(i, j)
                pe.wait_ge(s_pick0[j], i * 4 + 4)
                pe.wait_ge(s_xin[j], i * 16 + 16)
                ge(pe, s_x1, t - 1)
                nc.tensor.matmul(bank[j % 2], bd0[j], x_sb[j], start=True, stop=True).then_inc(s_mm0, 1)

            def turn1(i, j):
                i, j, t = tile(i, j)
                pe.wait_ge(s_x1, t + 1)
                ge(pe, s_x1T, t)
                transposes(bank[4], x1_sb[j]).then_inc(s_tx1, 1)

            def base(i, j):
                i, j, t = tile(i, j)
                pe.wait_ge(s_x1T, t + 1)
                pe.wait_ge(s_pick[j], i * 4 + 4)
                ge(pe, s_hT, t)
                for c in range(HC):
                    last = nc.tensor.matmul(bank[5][0:BT * RANK, 0:P], a4[j][:, c, :],
                                            x1T_sb[j][:, c * P:(c + 1) * P], start=(c == 0), stop=(c == HC - 1))
                last.then_inc(s_hmm, 1)
                pe.wait_ge(s_x1lo, t + 1)
                for c in range(HC):
                    rows, cols = slice(c * P, (c + 1) * P), slice(c * T, (c + 1) * T)
                    for m, (a, w) in enumerate(((x1T_hi, wb_hi), (x1T_hi, wb_lo), (x1T_lo, wb_hi))):
                        nc.tensor.matmul(bank[2 + j % 2], a[j % 2][:, rows], w[:, cols], start=(c == 0 and m == 0), stop=False)

            def own_adapters(i, j):
                i, j, t = tile(i, j)
                pe.wait_ge(s_hT, t + 1)
                pe.wait_ge(s_bin[j], i * 64 + 64)
                nc.tensor.matmul(bank[2 + j % 2], hT[j][0:BT * RANK + 1, :], b4[j][0:BT * RANK + 1, :], start=False, stop=True)\
                    .then_inc(s_mm1, 1)

            def turn2(i, j):
                i, j, t = tile(i, j)
                pe.wait_ge(s_x2, t + 1)
                ge(pe, s_x2lo, t - 1)
                transposes(bank[6 + j % 2], x2_sb[j]).then_inc(s_tx2, 1)

            def round1a(i, first, last):
                for j in range(4):
                    if not (last and j >= 2):
                        mix0(i, j + 2)
                    if not (last and j == 3):
                        turn1(i, j + 1)
                    if first and j == 0:
                        pe.wait_ge(s_wblo, HC)
                        pe.wait_ge(s_bias, 64)
                    base(i, j)
                    if not (first and j == 0):
                        turn2(i, j - 1)
                    own_adapters(i, j)

            pe.wait_ge(s_ones, 4)
            mix0(0, 0)
            mix0(0, 1)
            pe.wait_ge(s_const, 32)
            turn1(0, 0)
            round1a(0, True, False)
            with pe.Fori(1, NT // 4 - 1) as i:
                round1a(i, False, False)
            round1a(NT // 4 - 1, False, True)
            turn2(NT // 4 - 1, 3)

            def project(t, k):
                for c in range(HC):
                    rows, cols = slice(t * P, (t + 1) * P), slice(c * T, (c + 1) * T)
                    for m, (a, w) in enumerate(((x2T_hi, w_hi), (x2T_hi, w_lo), (x2T_lo, w_hi))):
                        last = nc.tensor.matmul(bank[t % 4], a[:, c, rows], w[k][:, cols],
                                                start=(c == 0 and m == 0), stop=(c == HC - 1 and m == 2))
                return last

            for j in range(VB):
                pe.wait_ge(s_wlo, (j + 1) * HC)
                for t in range(NT):
                    if j == 0:
                        pe.wait_ge(s_x2lo, t + 1)
                    ge(pe, s_vc, j * NT + t - 3)
                    project(t, j).then_inc(s_vp, 1)

            def project_qk(e, t, k):
                if t == 0:
                    pe.wait_ge(s_wlo, e * HC + (VB + 1) * HC)
                ge(pe, s_rot, e * NT + t - 3)
                project(t, k).then_inc(s_pj, 1)

            def turn_qk(e, t):
                pe.wait_ge(s_qr, e * (2 * NT) + 2 * t + 2)
                ge(pe, s_qT, e * NT + t - 1)
                transposes(bank[4 + t % 2], qr_sb[t % 4]).then_inc(s_tq, 1)

            def block_qk(e, k, last):
                for t in range(NT):
                    if t + LAG < NT:
                        project_qk(e, t + LAG, k)
                    elif not last:
                        project_qk(e + 1, t + LAG - NT, 1 - k)
                    turn_qk(e, t)
                    if last and t == NT - LAG:
                        score(0, 0)

            def score(n, u):
                pe.wait_ge(s_klo, n + 1)
                pe.wait_ge(s_qp, n + 1)
                ge(pe, s_mx, n - 1)
                halves = (slice(0, 9 * PSIZE), slice(9 * PSIZE, KW))
                for m, (q, k) in enumerate(((q_hi, k_hi), (q_hi, k_lo), (q_lo, k_hi))):
                    for at in halves:
                        last = nc.tensor.matmul(scores[u % 2][:, at], q[u % 2], k[u % 2][:, at],
                                                start=(m == 0), stop=(m == 2))
                last.then_inc(s_qk, 1)

            def turn_p(g, u):
                n = g * UG + u
                pe.wait_ge(s_p, n + 1)
                ge(pe, s_evA, n - 1)
                transposes(pT[u % 2], p_sb[u % 4]).then_inc(s_ta, 1)
                if u % 4 == 3:
                    pe.wait_ge(s_evA, n)
                    nc.tensor.transpose(pT[0][:, 0:P], po_sb[u // 4 % 2], ident[:]).then_inc(s_tb, 1)

            def values(g, u):
                n = g * UG + u
                b, j = u // HK % 2, u % 4
                if u % HK == 0:
                    pair = g * 2 + u // (2 * HK)
                    pe.wait_ge(s_v[b], pair * 64 + 64)
                    ge(pe, s_ost, g * BT + u // HK)
                elif j == 0:
                    pe.wait_ge(s_oev, g * BT + (u // HK + 1))
                pe.wait_ge(s_evA, n + 1)
                for m in range(4):
                    last = nc.tensor.matmul(oP[:, j * P:(j + 1) * P], v_sb[b][:, m, u % HK * D:(u % HK + 1) * D],
                                            pT_sb[u % 2][:, m * P:(m + 1) * P],
                                            start=(j == 0 and m == 0), stop=False)
                last.then_inc(s_pv, 1)
                if j == 3:
                    if u % HK == 3:
                        pe.wait_ge(s_vs[b], (g * 2 + u // (2 * HK)) * 64 + 64)
                    pe.wait_ge(s_evB, g * HK + (u // 4 + 1))
                    at = u // 4 % 2 * D
                    nc.tensor.matmul(oP, vo_sb[b][:, at:at + D], pTo_sb, start=False, stop=True).then_inc(s_po, 1)

            def split_product(dst, o, w, h, first, last):
                rows, cols = slice(h * P, (h + 1) * P), slice(h * T, (h + 1) * T)
                for m, (a, c) in enumerate(((0, 0), (0, 1), (1, 0))):
                    done = nc.tensor.matmul(dst, o[a][:, rows], w[c][:, cols], start=(first and m == 0), stop=(last and m == 2))
                return done

            def out_proj(g, h0, h1):
                if h0 == 0:
                    pe.wait_ge(s_oev, g * BT + BT)
                    pe.wait_ge(s_wolo, H2)
                for h in range(h0, h1):
                    last = split_product(yP, (oT_hi, oT_lo), (wo_hi, wo_lo), h, h == 0, h == H2 - 1)
                if h1 == H2:
                    last.then_inc(s_wo, 1)

            def step(g, u, before):
                n = g * UG + u
                fixed = isinstance(n, int)
                if not (fixed and n + 2 >= NU):
                    score(n + 2, u + 2)
                if u % 4:
                    turn_p(g, u)
                of = g if u >= UG - 2 else before
                if u in WO_AT and WO_AT[u] < H2 and of is not None:
                    out_proj(of, WO_AT[u], WO_AT[(u + 1) % UG])
                if u > 0:
                    values(g, u - 1)
                elif not (fixed and n == 0):
                    values(g - 1, UG - 1)
                if u % 4 == 0:
                    turn_p(g, u)

            pe.wait_ge(s_vc, VB * NT)
            for t in range(LAG):
                project_qk(0, t, 0)
            block_qk(0, 0, False)
            with pe.Fori(0, QKB // 2 - 1) as ee:
                block_qk(ee * 2 + 1, 1, False)
                block_qk(ee * 2 + 2, 0, False)
            block_qk(QKB - 1, 1, True)

            score(1, 1)
            pe.wait_ge(s_qT, QKB * NT)
            for u in range(ROT):
                step(0, u, None)
            with pe.Fori(0, NT - 1) as g:
                for u in range(ROT, UG):
                    step(g, u, None)
                for u in range(ROT):
                    step(g + 1, u, g)
            for u in range(ROT, UG):
                step(NT - 1, u, None)
            values(NT - 1, UG - 1)
            out_proj(NT - 1, WO_AT[0], H2)

            def out_proj3(g, i, first):
                pe.wait_ge(s_o3lo, g + 1)
                ge(pe, s_x3, g - 1)
                for h in range(H2):
                    if first:
                        pe.wait_ge(s_wolo, H2 + h + 1)
                    last = split_product(bank[i], (o3_hi[i], o3_lo[i]), (wo_hi, wo3_lo), h, h == 0, h == H2 - 1)
                last.then_inc(s_wo3, 1)

            def mix3(g, i):
                pe.wait_ge(s_x3, g + 1)
                pe.wait_ge(s_bd3[i], (g - i) * 2 + BT)
                nc.tensor.matmul(bank[2 + i], bd3[i], xy[i], start=True, stop=True).then_inc(s_l3, 1)

            out_proj3(0, 0, True)
            out_proj3(1, 1, False)
            mix3(0, 0)
            with pe.Fori(1, NT // 2) as gg:
                for i in range(2):
                    out_proj3(gg * 2 + i, i, False)
                    mix3(gg * 2 + (i - 1), 1 - i)
            mix3(NT - 1, 1)


def kernel(x, itok_B_0_15, itok_B_6_15, itok_Bx16_0_63, itok_B_207_1644, L0_cond_weights, L1_cond_base_weight,
           L1_cond_base_bias, L1_cond_lora_A_w, L1_cond_lora_B_w, L2_cond_Wq, L2_cond_Wk, L2_cond_Wv, L2_cond_Wo,
           L2_cond_q_norm_w, L2_cond_k_norm_w, L2_cond_k_cache, L2_cond_v_cache, L3_cond_weights):
    import concourse.bacc as bacc
    from concourse.bass_utils import run_bass_kernel_spmd

    def blocks(w, n):
        return np.asarray(w).reshape(n, T, HC, P).transpose(0, 3, 2, 1)

    bt = np.asarray(itok_Bx16_0_63)
    seq = np.asarray(itok_B_207_1644)
    of_row = np.arange(P) // C
    lora_a = np.asarray(L1_cond_lora_A_w).reshape(LORAS, RANK, HC, P).transpose(3, 0, 2, 1).reshape(P, LORAS, HC * RANK)
    arrays = {
        "x": np.asarray(x).reshape(NT, P, T),
        "cond_row": np.asarray(itok_B_0_15).reshape(1, B),
        "id_row": np.asarray(itok_B_6_15).reshape(1, B),
        "bt_row": bt.reshape(1, B * NPP),
        "idx_pages": np.repeat(bt.reshape(B, 4, 4).transpose(2, 0, 1).reshape(4, B * 4), PSIZE, axis=0),
        "seq_tok": seq.reshape(NT, BT)[:, of_row].T,
        "seq_all": np.repeat(seq.reshape(1, B), P, axis=0),
        "w0": np.tile(np.asarray(L0_cond_weights).transpose(1, 0, 2), (BT, 1, 1)),
        "w3": np.tile(np.asarray(L3_cond_weights).transpose(1, 0, 2), (BT, 1, 1)),
        "wb": np.asarray(L1_cond_base_weight).reshape(T, HC, P).transpose(2, 1, 0),
        "bias": np.asarray(L1_cond_base_bias).reshape(1, T),
        "lora_a": lora_a,
        "lora_b": np.asarray(L1_cond_lora_B_w).transpose(0, 2, 1),
        "wqk": np.concatenate([blocks(L2_cond_Wq, HK), blocks(L2_cond_Wk, HK // 4)]),
        "wv": blocks(L2_cond_Wv, VB),
        "wo": np.asarray(L2_cond_Wo).reshape(T, 2, H2, D).transpose(1, 3, 2, 0).reshape(2, D, H2 * T),
        "qn": np.repeat(np.asarray(L2_cond_q_norm_w).reshape(1, D), P, axis=0),
        "kn": np.repeat(np.asarray(L2_cond_k_norm_w).reshape(1, D), P, axis=0),
        "kT_cache": np.asarray(L2_cond_k_cache).transpose(0, 3, 2, 1).reshape(PAGES, D, HK * PSIZE),
        "v_cache": np.asarray(L2_cond_v_cache).reshape(PAGES * PSIZE, HK * D),
        "ident_c": np.eye(P, dtype=np.float32),
        "iota_c": np.tile(np.arange(L, dtype=np.float32), (P, 1)),
        "row_c": (np.arange(P) % C).astype(np.float32).reshape(P, 1),
        "invf_c": np.tile((1.0 / 10000.0 ** (np.arange(0, D, 2) / D)).astype(np.float32), (P, 1)),
        "hmask_c": np.repeat(np.repeat(np.eye(BT, dtype=np.float32), RANK, axis=0), C, axis=1),
    }
    arrays = {k: np.ascontiguousarray(v) for k, v in arrays.items()}
    nc = bacc.Bacc("TRN2", target_bir_lowering=False, num_devices=1)
    aps = {k: nc.dram_tensor(k, v.shape, mybir.dt.from_np(v.dtype), kind="ExternalInput").ap() for k, v in arrays.items()}
    aps["out"] = nc.dram_tensor("out", (NT, P, T), F32, kind="ExternalOutput").ap()
    build(nc, **aps)
    r = run_bass_kernel_spmd(nc, [arrays], core_ids=[0])
    return np.asarray(r.results[0]["out"]).reshape(B, C, T)
```
